# Optimizing a Trainium2 kernel written in Bass

```python
import numpy as np
import jax
import jax.numpy as jnp

def _softmax(x, axis=-1):
    return jax.nn.softmax(x, axis=axis)

def _gelu(x):
    return jax.nn.gelu(x, approximate=True)

def _silu(x):
    return jax.nn.silu(x)

def _sigmoid(x):
    return jax.nn.sigmoid(x)

def _layernorm(x, axis=-1, eps=1e-05):
    m = jnp.mean(x, axis=axis, keepdims=True)
    v = jnp.var(x, axis=axis, keepdims=True)
    return (x - m) / jnp.sqrt(v + eps)

def _scatter_add(tgt, idx, src, axis=0):
    return tgt.at[idx].add(src)

def _segment_sum(src, seg, n):
    return jax.ops.segment_sum(src, seg, n)
kernel_name = 'mk_adj_ffn_d1_adj_r2_ce1392'

def setup_inputs(seed: int=0):
    np.random.seed(seed)
    _w = jnp.asarray

    def _rec_inputs():
        import jax
        import jax.numpy as jnp
        _gk = jax.random.key(seed)
        x = -0.0006128 + 1 * jax.random.normal(jax.random.fold_in(_gk, 1), (64, 128, 128), jnp.float32)
        _w = (1.0 + jnp.arange(128, dtype=jnp.float32)) ** (-0.5)
        _w = _w / _w.mean()
        _pij = jnp.clip(0.125 * _w[:, None] * _w[None, :], 0.0, 1.0)
        _a = jax.random.uniform(jax.random.fold_in(_gk, 2), (64, 128, 128)) < _pij
        adj = _a.astype(jnp.int32)
        return (x, adj)
    x, adj = _rec_inputs()

    def _L0_gnn_setup():
        import jax, jax.numpy as jnp
        import numpy as np
        D = 128
        H = 8
        HD = D // H
        key = jax.random.key(seed)
        ks = jax.random.split(key, 10)
        BT, N = (32, 200)
        s = 1.0 / np.sqrt(D)
        return {'x': jax.random.normal(ks[0], (BT, N, D), dtype=jnp.float32), 'adj': jax.random.randint(ks[1], (BT, N, N), 0, 2, dtype=jnp.int32), 'Wq': jax.random.normal(ks[2], (D, D), dtype=jnp.float32) * s, 'bq': jnp.zeros((D,), dtype=jnp.float32), 'Wk': jax.random.normal(ks[3], (D, D), dtype=jnp.float32) * s, 'bk': jnp.zeros((D,), dtype=jnp.float32), 'Wv': jax.random.normal(ks[4], (D, D), dtype=jnp.float32) * s, 'bv': jnp.zeros((D,), dtype=jnp.float32), 'Wo': jax.random.normal(ks[5], (D, D), dtype=jnp.float32) * s, 'bo': jnp.zeros((D,), dtype=jnp.float32)}
    _L0_gnn_all = _L0_gnn_setup()
    _L0_gnn_in = {k: v for k, v in _L0_gnn_all.items() if k in ('Wq', 'bq', 'Wk', 'bk', 'Wv', 'bv', 'Wo', 'bo')}
    del _L0_gnn_all

    def _L0_ffn_setup():
        import jax, jax.numpy as jnp
        import numpy as np
        E = 8
        K = 2
        D = 128
        H = 256
        DOUT = 128
        EPS = 1e-05
        key = jax.random.key(seed)
        ks = jax.random.split(key, 9)
        s = 0.02
        return {'x': jax.random.normal(ks[0], (4, 4096, D), jnp.float32), 'gamma': 1.0 + 0.05 * jax.random.normal(ks[1], (D,), jnp.float32), 'beta': 0.05 * jax.random.normal(ks[2], (D,), jnp.float32), 'Wr': 0.01 * jax.random.normal(ks[3], (D, E), jnp.float32), 'br': jnp.zeros((E,), jnp.float32), 'W1': s * jax.random.normal(ks[4], (E, D, H), jnp.float32), 'b1': s * jax.random.normal(ks[5], (E, H), jnp.float32), 'W2': s * jax.random.normal(ks[6], (E, H, DOUT), jnp.float32), 'b2': s * jax.random.normal(ks[7], (E, DOUT), jnp.float32)}
    _L0_ffn_all = _L0_ffn_setup()
    _L0_ffn_in = {k: v for k, v in _L0_ffn_all.items() if k in ('gamma', 'beta', 'Wr', 'br', 'W1', 'b1', 'W2', 'b2')}
    del _L0_ffn_all
    return {'x': x, 'adj': adj, 'L0_gnn_Wq': _L0_gnn_in['Wq'], 'L0_gnn_bq': _L0_gnn_in['bq'], 'L0_gnn_Wk': _L0_gnn_in['Wk'], 'L0_gnn_bk': _L0_gnn_in['bk'], 'L0_gnn_Wv': _L0_gnn_in['Wv'], 'L0_gnn_bv': _L0_gnn_in['bv'], 'L0_gnn_Wo': _L0_gnn_in['Wo'], 'L0_gnn_bo': _L0_gnn_in['bo'], 'L0_ffn_gamma': _L0_ffn_in['gamma'], 'L0_ffn_beta': _L0_ffn_in['beta'], 'L0_ffn_Wr': _L0_ffn_in['Wr'], 'L0_ffn_br': _L0_ffn_in['br'], 'L0_ffn_W1': _L0_ffn_in['W1'], 'L0_ffn_b1': _L0_ffn_in['b1'], 'L0_ffn_W2': _L0_ffn_in['W2'], 'L0_ffn_b2': _L0_ffn_in['b2']}

def reference(x, adj, L0_gnn_Wq, L0_gnn_bq, L0_gnn_Wk, L0_gnn_bk, L0_gnn_Wv, L0_gnn_bv, L0_gnn_Wo, L0_gnn_bo, L0_ffn_gamma, L0_ffn_beta, L0_ffn_Wr, L0_ffn_br, L0_ffn_W1, L0_ffn_b1, L0_ffn_W2, L0_ffn_b2):
    import jax
    import jax.numpy as jnp

    def _L0_gnn_ref(x, adj, Wq, bq, Wk, bk, Wv, bv, Wo, bo):
        import jax, jax.numpy as jnp
        import numpy as np
        D = 128
        H = 8
        HD = D // H
        BT, N, _ = x.shape

        def heads(t):
            return t.reshape(BT, N, H, HD).transpose(0, 2, 1, 3)
        q = heads(x @ Wq + bq)
        k = heads(x @ Wk + bk)
        v = heads(x @ Wv + bv)
        scores = jnp.einsum('bhnd,bhmd->bhnm', q, k) / np.sqrt(HD)
        mask = (adj == 0)[:, None, :, :]
        scores = jnp.where(mask, -jnp.inf, scores)
        attn = jax.nn.softmax(scores, axis=-1)
        ctx = jnp.einsum('bhnm,bhmd->bhnd', attn, v)
        ctx = ctx.transpose(0, 2, 1, 3).reshape(BT, N, D)
        return ctx @ Wo + bo

    def _L0_ffn_ref(x, gamma, beta, Wr, br, W1, b1, W2, b2):
        import jax, jax.numpy as jnp
        import numpy as np
        E = 8
        K = 2
        D = 128
        H = 256
        DOUT = 128
        EPS = 1e-05
        mu = jnp.mean(x, axis=-1, keepdims=True)
        var = jnp.mean(jnp.square(x - mu), axis=-1, keepdims=True)
        xn = (x - mu) * jax.lax.rsqrt(var + EPS) * gamma + beta
        logits = jnp.einsum('bsd,de->bse', xn, Wr) + br
        top_vals, top_idx = jax.lax.top_k(logits, K)
        w = jax.nn.softmax(top_vals, axis=-1)
        w_full = jnp.einsum('bsk,bske->bse', w, jax.nn.one_hot(top_idx, E, dtype=w.dtype))
        y = jnp.zeros(x.shape[:-1] + (DOUT,), x.dtype)
        for e in range(E):
            h = jax.nn.gelu(jnp.einsum('bsd,dh->bsh', xn, W1[e]) + b1[e], approximate=False)
            y_e = jnp.einsum('bsh,hd->bsd', h, W2[e]) + b2[e]
            y = y + y_e * w_full[..., e, None]
        return y
    x = x + _L0_gnn_ref(_layernorm(x, axis=-1), adj, L0_gnn_Wq, L0_gnn_bq, L0_gnn_Wk, L0_gnn_bk, L0_gnn_Wv, L0_gnn_bv, L0_gnn_Wo, L0_gnn_bo)
    x = x + _L0_ffn_ref(_layernorm(x, axis=-1), L0_ffn_gamma, L0_ffn_beta, L0_ffn_Wr, L0_ffn_br, L0_ffn_W1, L0_ffn_b1, L0_ffn_W2, L0_ffn_b2)
    return x

_drawn_inputs = setup_inputs


def setup_inputs(seed=0):
    import zlib

    import numpy as np

    out = dict(_drawn_inputs(seed))
    spreads = {'L0_gnn_bq': (0.0, 0.294),
     'L0_gnn_bk': (0.0, 0.8),
     'L0_gnn_bv': (0.0, 0.1),
     'L0_gnn_bo': (0.0, 0.1),
     'L0_ffn_br': (0.0, 0.286)}
    factors = {'L0_ffn_gamma': 8.0,
     'L0_ffn_beta': 8.0,
     'L0_ffn_Wr': 3.761,
     'L0_ffn_b1': 8.0,
     'L0_ffn_b2': 4.501}
    for name, (base, spread) in spreads.items():
        noise = np.random.default_rng([zlib.crc32(name.encode()), seed]).standard_normal(out[name].shape)
        drawn = base * np.exp(spread * noise) if base else spread * noise
        out[name] = jnp.asarray(drawn.astype(out[name].dtype))
    for name, factor in factors.items():
        out[name] = (out[name] * factor).astype(out[name].dtype)
    return out
```

```python
from contextlib import ExitStack

import concourse.bass as bass
from concourse import mybir

F32 = mybir.dt.float32
BF16 = mybir.dt.bfloat16
I32 = mybir.dt.int32
U32 = mybir.dt.uint32
ALU = mybir.AluOpType
ACT = mybir.ActivationFunctionType
AX = mybir.AxisListType.X

MASKED = -1.0e30
EMPTY_ROW = -5.0e29
HUGE = 3.0e38
EPS = 1e-05
HEADS = 8
SLOT = 32
QUAD = 4
TURN = 8


def wait_from_one(engine, semaphore, value):
    if isinstance(value, int) and value <= 0:
        return
    engine.wait_ge(semaphore, value)


def build(nc, x, adj, Wq, bq, Wk, bk, Wv, bv, Wo, bo, gamma, beta, Wr, br, W1, b1, W2, b2, out):
    G, N, D = x.shape
    E, _, HID = W1.shape
    HD = D // HEADS
    CH = HID // 128
    HALF = HEADS // 2
    TURNS = G // TURN
    QUADS = G // QUAD
    assert N == 128 and D == 128 and W2.shape[2] == D and G % TURN == 0 and E == 8

    with ExitStack() as ctx:
        def sb(name, shape, dt=F32):
            return ctx.enter_context(nc.sbuf_tensor(name, shape, dt))

        def sem(name):
            return ctx.enter_context(nc.semaphore(name))

        X = sb("X", [128, G, D])
        ident = sb("ident", [128, 128])
        identb = sb("identb", [128, 128], BF16)
        ones_row = sb("ones_row", [1, 128])
        wq = sb("wq", [D, D])
        wk = sb("wk", [D, D])
        wv = sb("wv", [D, D])
        wo = sb("wo", [D, D])
        bq_col = sb("bq_col", [D, 1])
        bk_col = sb("bk_col", [D, 1])
        bv_col = sb("bv_col", [D, 1])
        bv_wide = sb("bv_wide", [D, 128])
        bo_row = sb("bo_row", [1, D])
        attn_bias = sb("attn_bias", [128, D])
        gamma_col = sb("gamma_col", [D, 1])
        beta_col = sb("beta_col", [D, 1])
        wr = sb("wr", [D, E])
        br_row = sb("br_row", [1, E])
        w1 = sb("w1", [D, E, HID])
        w2 = sb("w2", [128, E, CH, D])
        b1_col = sb("b1_col", [128, E, CH])
        b2_rows = sb("b2_rows", [E, D])
        iota_e = sb("iota_e", [128, E])
        stats = sb("stats", [128, G, 6])
        mean = sb("mean", [128, G])
        rstd = sb("rstd", [128, G])
        tmp_a = sb("tmp_a", [128, G])
        tmp_b = sb("tmp_b", [128, G])
        adj_raw = sb("adj_raw", [128, 2, QUAD, N], I32)
        mask_bias = sb("mask_bias", [128, 2, QUAD, N], BF16)
        xhat = sb("xhat", [128, QUAD, D])
        xT = sb("xT", [D, QUAD * N])
        qT = sb("qT", [D, 2, QUAD * N])
        kT = sb("kT", [D, QUAD * N])
        k_diag = sb("k_diag", [D, 2, QUAD, HEADS, N])
        v_slots = sb("v_slots", [128, 2, QUAD, HEADS, SLOT])
        probs = sb("probs", [128, 2, HEADS, N])
        probsT = sb("probsT", [128, HEADS, N])
        row_max = sb("row_max", [128, TURN, HEADS])
        no_edge = sb("no_edge", [128, G])
        ctxT_raw = sb("ctxT_raw", [128, 2 * N])
        rden = sb("rden", [128, HEADS])
        ctxn = sb("ctxn", [128, HEADS, HD])
        ctxT = sb("ctxT", [D, N])
        z = sb("z", [128, QUAD, D])
        xnT = sb("xnT", [D, 2, QUAD * N])
        logit = sb("logit", [128, QUAD, E])
        top = sb("top", [128, QUAD, E])
        top_i = sb("top_i", [128, QUAD, E], U32)
        top_f = sb("top_f", [128, QUAD, 2])
        gap = sb("gap", [128, QUAD])
        tanh_gap = sb("tanh_gap", [128, QUAD])
        gates = sb("gates", [128, QUAD, 2])
        pick = sb("pick", [128, 2, QUAD, E])
        w_full = sb("w_full", [128, 2, QUAD, E])
        w_fullT = sb("w_fullT", [E, QUAD, N])
        hid = sb("hid", [128, 2, CH, QUAD * N])
        acc = sb("acc", [128, 2, QUAD, D])

        P = ctx.enter_context(nc.psum_tensor("P", [128, 8, 512], F32))
        P_SCORES, P_T, P_PREP, P_CTX = 0, 4, 6, 7

        block = ctx.enter_context(nc.Block())

        s_w1 = sem("s_attention_weights_loaded")
        s_w2 = sem("s_expert_weights_loaded")
        s_x = [sem(f"s_x_loaded_{t}") for t in range(TURNS)]
        s_ones = sem("s_ones")
        s_ident0 = sem("s_ident_zeroed")
        s_const = sem("s_constants")
        s_v_ones = sem("s_v_slots_preset")
        s_kd_zero = sem("s_k_diag_zeroed")
        s_stat = sem("s_stats1")
        s_ln = sem("s_ln_chain")
        s_var = sem("s_var_ready")
        s_std = sem("s_std_ready")
        s_rstd = sem("s_rstd_ready")
        s_ab_mm = sem("s_attn_bias_product")
        s_ab = sem("s_attn_bias")
        s_bvw = sem("s_bv_wide")
        s_adj = [sem(f"s_adj_loaded_{b}") for b in range(2)]
        s_mask = sem("s_mask_bias")
        s_centred = sem("s_x_less_mean")
        s_xhat = sem("s_xhat")
        s_xhatT = sem("s_xhatT")
        s_xT = sem("s_xT")
        s_qmm = sem("s_q_product")
        s_q = sem("s_qT")
        s_kmm = sem("s_k_product")
        s_k = sem("s_kT")
        s_kd = [sem(f"s_k_diag_{b}") for b in range(2)]
        s_vmm = sem("s_v_product")
        s_v = sem("s_v_slots")
        s_sc = sem("s_scores")
        s_max = sem("s_row_max")
        s_edge = sem("s_no_edge")
        s_nan = sem("s_nan_rows")
        s_sub = sem("s_scores_less_max")
        s_exp = sem("s_probs")
        s_pT = sem("s_probsT_psum")
        s_pTe = sem("s_probsT")
        s_pv = sem("s_context_product")
        s_cr = sem("s_ctxT_raw")
        s_back = sem("s_context_back")
        s_rden = sem("s_rden")
        s_norm = sem("s_ctxn")
        s_cT = sem("s_ctxT_psum")
        s_cTe = sem("s_ctxT")
        s_wo = sem("s_out_product")
        s_xc = sem("s_x_plus_bias")
        s_res = sem("s_residual")
        s_st2 = sem("s_stats2")
        s_rstd2 = sem("s_rstd2_ready")
        s_z = sem("s_z")
        s_zT = sem("s_zT")
        s_xn = sem("s_xnT")
        s_lg = sem("s_logits_product")
        s_l = sem("s_logits")
        s_rt = sem("s_route_chain")
        s_gap = sem("s_gap")
        s_tanh = sem("s_tanh")
        s_wf = sem("s_w_full")
        s_wfT = sem("s_w_fullT_psum")
        s_wfTe = sem("s_w_fullT")
        s_b2 = sem("s_b2_product")
        s_acc0 = sem("s_acc_started")
        s_h = sem("s_hidden_product")
        s_g = sem("s_gelu")
        s_y = sem("s_expert_product")
        s_acc = sem("s_expert_added")
        s_out = [sem(f"s_out_{b}") for b in range(2)]

        n_attn_weights, n_expert_weights = 8, 9

        def col(ap):
            return ap.rearrange("(p a) -> p a", a=1)

        def row(ap):
            return ap.rearrange("(a n) -> a n", a=1)

        adj_q = adj.rearrange("(q k) n m -> q n k m", k=QUAD)
        out_q = out.rearrange("(q k) n d -> q n k d", k=QUAD)

        def exists(g):
            return not isinstance(g, int) or 0 <= g < G

        @block.sync
        def _(sp):
            x_t = x.rearrange("(t g) n d -> t n g d", g=TURN)
            sp.dma_start(X[:, 0:TURN, :], x_t[0]).then_inc(s_x[0], 16)
            sp.dma_start(adj_raw[:, 0], adj_q[0]).then_inc(s_adj[0], 16)
            sp.dma_start(adj_raw[:, 1], adj_q[1]).then_inc(s_adj[1], 16)
            for dst, src in ((wq[:, :], Wq), (wk[:, :], Wk), (wv[:, :], Wv), (wo[:, :], Wo),
                             (bq_col[:, :], col(bq)), (bk_col[:, :], col(bk)), (bv_col[:, :], col(bv)),
                             (bo_row[:, :], row(bo))):
                sp.dma_start(dst, src).then_inc(s_w1, 16)
            for t in range(1, TURNS):
                sp.dma_start(X[:, t * TURN:(t + 1) * TURN, :], x_t[t]).then_inc(s_x[t], 16)
            for dst, src in ((gamma_col[:, :], col(gamma)), (beta_col[:, :], col(beta)), (wr[:, :], Wr),
                             (br_row[:, :], row(br)), (w1[:, :, :], W1.rearrange("e d h -> d e h")),
                             (b2_rows[:, :], b2)):
                sp.dma_start(dst, src).then_inc(s_w2, 16)
            for c in range(CH):
                sp.dma_start(w2[:, :, c, :], W2[:, c * 128:(c + 1) * 128, :].rearrange("e p d -> p e d")).then_inc(s_w2, 16)
            sp.dma_start(b1_col[:, :, :].rearrange("p e c -> p (e c)"), b1.rearrange("e (c p) -> p (e c)", p=128),
                         allow_slow_non_contiguous=True).then_inc(s_w2, 16)

            def spread_k(turn, j):
                sp.wait_ge(s_kd_zero, 2)
                sp.wait_ge(s_k, turn * 2 + j + 1)
                for h in range(HEADS):
                    rows = slice(h * HD, (h + 1) * HD)
                    sp.dma_start(k_diag[rows, j, :, h, :], kT[rows, :].rearrange("p (k n) -> p k n", k=QUAD)).then_inc(s_kd[j], 16)

            sp.wait_ge(s_kd_zero, 2)
            spread_k(0, 0)

            def turn_sp(t, last):
                for j in range(2):
                    if not (last and j == 1):
                        spread_k(t + (j + 1) // 2, (j + 1) % 2)
                    if not last:
                        sp.wait_ge(s_kd_zero, 2)
                        sp.wait_ge(s_mask, t * 2 + j + 1)
                        sp.dma_start(adj_raw[:, j], adj_q[t * 2 + (j + 2)]).then_inc(s_adj[j], 16)

            turn_sp(0, False)
            with sp.Fori(1, TURNS - 1) as t:
                turn_sp(t, False)
            turn_sp(TURNS - 1, True)

            def store(q, b):
                sp.wait_ge(s_kd_zero, 2)
                sp.wait_ge(s_acc, q * (E * QUAD) + E * QUAD)
                sp.dma_start(out_q[q], acc[:, b]).then_inc(s_out[b], 16)

            with sp.Fori(0, QUADS // 2) as p:
                store(p * 2, 0)
                store(p * 2 + 1, 1)
            for b in range(2):
                sp.wait_ge(s_out[b], 16 * (QUADS // 2))

        @block.gpsimd
        def _(pool):
            nc.gpsimd.memset(ident[:, :], 0.0).then_inc(s_ident0, 1)
            nc.gpsimd.memset(identb[:, :], 0.0).then_inc(s_ident0, 1)
            pool.wait_ge(s_ident0, 2)
            for m in (ident, identb):
                nc.gpsimd.affine_select(out=m[:, :], in_=m[:, :], compare_op=ALU.not_equal, fill=1.0, base=0,
                                        pattern=[[-1, 128]], channel_multiplier=1).then_inc(s_const, 1)
            nc.gpsimd.iota(iota_e[:, :], pattern=[[1, E]], base=0, channel_multiplier=0,
                           allow_small_or_imprecise_dtypes=True).then_inc(s_const, 1)

            def normalise(t, j):
                quad = bass.ds(t * TURN + QUAD * j, QUAD)
                wide = [128, QUAD, D]
                pool.wait_ge(s_rstd, 1)
                wait_from_one(pool, s_xhatT, t * 2 + j)
                nc.gpsimd.tensor_tensor(xhat[:, :, :], X[:, quad, :], mean[:, quad].unsqueeze(2).to_broadcast(wide),
                                        ALU.subtract).then_inc(s_centred, 1)
                pool.wait_ge(s_rstd, 1)
                pool.wait_ge(s_centred, t * 2 + j + 1)
                nc.gpsimd.tensor_tensor(xhat[:, :, :], xhat[:, :, :], rstd[:, quad].unsqueeze(2).to_broadcast(wide),
                                        ALU.mult).then_inc(s_xhat, 1)
                pool.wait_ge(s_ab, 1)
                nc.gpsimd.tensor_tensor(X[:, quad, :], X[:, quad, :], attn_bias[:, :].unsqueeze(1).to_broadcast(wide),
                                        ALU.add).then_inc(s_xc, 1)

            normalise(0, 0)
            normalise(0, 1)

            def turn_pool(t, last):
                if not last:
                    for j in range(2):
                        normalise(t + 1, j)

            turn_pool(0, False)
            with pool.Fori(1, TURNS - 1) as t:
                turn_pool(t, False)
            turn_pool(TURNS - 1, True)

        @block.tensor
        def _(pe):
            mm = nc.tensor.matmul

            pe.wait_ge(s_w1, 16 * n_attn_weights)
            pe.wait_ge(s_bvw, 1)
            pe.wait_ge(s_ones, 1)
            pe.wait_ge(s_const, 3)
            mm(P[:, P_CTX, 0:D], bv_wide[:, :], wo[:, :], start=True, stop=False)
            mm(P[:, P_CTX, 0:D], ones_row[:, :], bo_row[:, :], start=False, stop=True).then_inc(s_ab_mm, 1)

            def prep_xT(t, j):
                pe.wait_ge(s_xhat, t * 2 + j + 1)
                wait_from_one(pe, s_v, t * 2 + j)
                for k in range(QUAD):
                    last = nc.tensor.transpose(P[:, P_PREP, k * N:(k + 1) * N], xhat[:, k, :], ident[:, :])
                last.then_inc(s_xhatT, 1)

            def prep_q(t, j):
                pe.wait_ge(s_xT, t * 2 + j + 1)
                mm(P[:, P_PREP, :], wq[:, :], xT[:, :], start=True, stop=True).then_inc(s_qmm, 1)

            def prep_k(t, j):
                pe.wait_ge(s_q, t * 2 + j + 1)
                mm(P[:, P_PREP, :], wk[:, :], xT[:, :], start=True, stop=True).then_inc(s_kmm, 1)

            def prep_v(t, j):
                pe.wait_ge(s_k, t * 2 + j + 1)
                for k in range(QUAD):
                    last = mm(P[:, P_PREP, k * N:(k + 1) * N], xT[:, k * N:(k + 1) * N], wv[:, :], start=True, stop=True)
                last.then_inc(s_vmm, 1)

            def scores(t, n, half):
                t, n = t + n // TURN, n % TURN
                j, k = n // QUAD, n % QUAD
                bank = P_SCORES + 2 * (n % 2) + half
                if half == 0:
                    wait_from_one(pe, s_sub, t * TURN + (n - 1))
                    pe.wait_ge(s_mask, t * 2 + j + 1)
                    pe.wait_ge(s_q, t * 2 + j + 1)
                    pe.wait_ge(s_kd[j], t * (16 * HEADS) + 16 * HEADS)
                bias = mask_bias[:, j, k, :].unsqueeze(1).to_broadcast([128, HALF, N])
                mm(P[:, bank, :].rearrange("p (h m) -> p h m", h=HALF), identb[:, :], bias, start=True, stop=False)
                mm(P[:, bank, :], qT[:, j, k * N:(k + 1) * N],
                   k_diag[:, j, k, half * HALF:(half + 1) * HALF, :].rearrange("p h m -> p (h m)"),
                   start=False, stop=True).then_inc(s_sc, 1)

            def turn_probs(t, n):
                pe.wait_ge(s_exp, t * TURN + n + 1)
                for half in range(2):
                    wait_from_one(pe, s_pTe, (t * TURN + n) * 2 + (half - 1))
                    for h in range(HALF):
                        last = nc.tensor.transpose(P[:, P_T + half, h * N:(h + 1) * N], probs[:, n % 2, half * HALF + h, :], ident[:, :])
                    last.then_inc(s_pT, 1)

            def context(t, n):
                pe.wait_ge(s_pTe, (t * TURN + n) * 2 + 2)
                pe.wait_ge(s_v, t * 2 + n // QUAD + 1)
                wait_from_one(pe, s_res, t * TURN + n)
                for h in range(HEADS):
                    slot, group = h % HALF, h // HALF
                    last = mm(P[slot * SLOT:(slot + 1) * SLOT, P_CTX, group * N:(group + 1) * N],
                              v_slots[:, n // QUAD, n % QUAD, h, :], probsT[:, h, :], start=True, stop=True,
                              tile_position=(0, slot * SLOT))
                last.then_inc(s_pv, 1)

            def context_back(g):
                pe.wait_ge(s_cr, g + 1)
                for group in range(2):
                    last = nc.tensor.transpose(P[:, P_CTX, group * 128:(group + 1) * 128], ctxT_raw[:, group * N:(group + 1) * N], ident[:, :])
                last.then_inc(s_back, 1)

            def context_turn(g):
                pe.wait_ge(s_norm, g + 1)
                nc.tensor.transpose(P[:, P_CTX, 0:N], ctxn[:, :, :].rearrange("p h d -> p (h d)"), ident[:, :]).then_inc(s_cT, 1)

            def project(g):
                pe.wait_ge(s_cTe, g + 1)
                mm(P[:, P_CTX, 0:D], ctxT[:, :], wo[:, :], start=True, stop=True).then_inc(s_wo, 1)

            def turn_pe(t, first, last):
                for n in range(TURN):
                    prev = not (first and n == 0)
                    more = not (last and n + 2 >= TURN)
                    turn_probs(t, n)
                    if prev:
                        context_back(t * TURN + (n - 1))
                    if more:
                        scores(t, n + 2, 0)
                    if prev:
                        context_turn(t * TURN + (n - 1))
                    if more:
                        scores(t, n + 2, 1)
                    if prev:
                        project(t * TURN + (n - 1))
                    j, k = n // QUAD, n % QUAD
                    one, two = (t + (j + 1) // 2, (j + 1) % 2), (t + 1, j)
                    if k == 0 and not (last and j == 1):
                        prep_k(*one)
                    if k == 1 and not (last and j == 1):
                        prep_v(*one)
                    if k == 2 and not last:
                        prep_xT(*two)
                    if k == 3 and not last:
                        prep_q(*two)
                    context(t, n)

            prep_xT(0, 0)
            prep_q(0, 0)
            prep_k(0, 0)
            prep_v(0, 0)
            prep_xT(0, 1)
            prep_q(0, 1)
            for n in range(2):
                for half in range(2):
                    scores(0, n, half)
            turn_pe(0, True, False)
            with pe.Fori(1, TURNS - 1) as t:
                turn_pe(t, False, False)
            turn_pe(TURNS - 1, False, True)
            context_back(G - 1)
            context_turn(G - 1)
            project(G - 1)

            pe.wait_ge(s_res, G)
            pe.wait_ge(s_w2, 16 * n_expert_weights)

            def front(q, b):
                pe.wait_ge(s_z, q + 1)
                wait_from_one(pe, s_xn, q)
                for k in range(QUAD):
                    last = nc.tensor.transpose(P[:, 5, k * N:(k + 1) * N], z[:, k, :], ident[:, :])
                last.then_inc(s_zT, 1)
                pe.wait_ge(s_xn, q + 1)
                wait_from_one(pe, s_wfTe, q)
                for k in range(QUAD):
                    mm(P[:, 6, k * E:(k + 1) * E], xnT[:, b, k * N:(k + 1) * N], wr[:, :], start=True, stop=False)
                    last = mm(P[:, 6, k * E:(k + 1) * E], ones_row[:, :], br_row[:, :], start=False, stop=True)
                last.then_inc(s_lg, 1)
                pe.wait_ge(s_wf, q + 1)
                for k in range(QUAD):
                    last = nc.tensor.transpose(P[0:E, 6, k * N:(k + 1) * N], w_full[:, b, k, :], ident[:, :])
                last.then_inc(s_wfT, 1)
                pe.wait_ge(s_wfTe, q + 1)
                wait_from_one(pe, s_acc0, q)
                for k in range(QUAD):
                    last = mm(P[:, 7, k * D:(k + 1) * D], w_fullT[:, k, :], b2_rows[:, :], start=True, stop=True)
                last.then_inc(s_b2, 1)

            def hidden(q, b, e):
                for c in range(CH):
                    wait_from_one(pe, s_g, q * (E * CH) + (e * CH + c - 1))
                    mm(P[:, (e * CH + c) % 2, :], w1[:, e, c * 128:(c + 1) * 128], xnT[:, b, :], start=True, stop=True).then_inc(s_h, 1)

            def result(q, e):
                pe.wait_ge(s_g, q * (E * CH) + (e * CH + CH))
                wait_from_one(pe, s_acc, q * (E * QUAD) + QUAD * (e - 1))
                for c in range(CH):
                    for k in range(QUAD):
                        last = mm(P[:, 3 + e % 2, k * D:(k + 1) * D], hid[:, e % 2, c, k * N:(k + 1) * N], w2[:, e, c, :],
                                  start=(c == 0 and k == 0), stop=(c == CH - 1), skip_group_check=True)
                last.then_inc(s_y, 1)

            def quad_pe(q, b):
                front(q, b)
                hidden(q, b, 0)
                for e in range(E):
                    if e + 1 < E:
                        hidden(q, b, e + 1)
                    result(q, e)

            quad_pe(0, 0)
            quad_pe(1, 1)
            with pe.Fori(1, QUADS // 2) as p:
                quad_pe(p * 2, 0)
                quad_pe(p * 2 + 1, 1)

        @block.scalar
        def _(act):
            fn = nc.scalar.activation
            act.wait_ge(s_w1, 16 * n_attn_weights)
            act.wait_ge(s_var, 1)
            fn(tmp_b[:, :], tmp_a[:, :], ACT.Sqrt).then_inc(s_std, 1)

            def prep_xT(t, j):
                act.wait_ge(s_xhatT, t * 2 + j + 1)
                wait_from_one(act, s_vmm, t * 2 + j)
                fn(xT[:, :], P[:, P_PREP, :], ACT.Identity).then_inc(s_xT, 1)

            def prep_q(t, j):
                act.wait_ge(s_qmm, t * 2 + j + 1)
                fn(qT[:, j, :], P[:, P_PREP, :], ACT.Identity, bias=bq_col[:, 0:1]).then_inc(s_q, 1)

            def prep_k(t, j):
                act.wait_ge(s_kmm, t * 2 + j + 1)
                if not (isinstance(t, int) and t == 0 and j == 0):
                    act.wait_ge(s_kd[1 - j], (t + (j - 1)) * (16 * HEADS) + 16 * HEADS if j == 0 else t * (16 * HEADS) + 16 * HEADS)
                fn(kT[:, :], P[:, P_PREP, :], ACT.Identity, bias=bk_col[:, 0:1]).then_inc(s_k, 1)

            def exps(t, n):
                act.wait_ge(s_sub, t * TURN + n + 1)
                p = probs[:, n % 2].rearrange("p h m -> p (h m)")
                fn(p, p, ACT.Exp, scale=float(HD) ** -0.5).then_inc(s_exp, 1)

            def probs_out(t, n):
                wait_from_one(act, s_pv, t * TURN + n)
                for half in range(2):
                    act.wait_ge(s_pT, (t * TURN + n) * 2 + half + 1)
                    fn(probsT[:, half * HALF:(half + 1) * HALF, :].rearrange("p h m -> p (h m)"), P[:, P_T + half, :], ACT.Identity).then_inc(s_pTe, 1)

            def context_out(g):
                act.wait_ge(s_cT, g + 1)
                fn(ctxT[:, :], P[:, P_CTX, 0:N], ACT.Identity).then_inc(s_cTe, 1)

            def raw_out(t, n):
                act.wait_ge(s_pv, t * TURN + n + 1)
                fn(ctxT_raw[:, :], P[:, P_CTX, 0:2 * N], ACT.Identity).then_inc(s_cr, 1)

            def turn_act(t, first, last):
                for n in range(TURN):
                    probs_out(t, n)
                    if not (first and n == 0):
                        context_out(t * TURN + (n - 1))
                    if not (last and n + 1 >= TURN):
                        exps(t + (n + 1) // TURN, (n + 1) % TURN)
                    j, k = n // QUAD, n % QUAD
                    if k == 0 and not (last and j == 1):
                        prep_k(t + (j + 1) // 2, (j + 1) % 2)
                    if k == 2 and not last:
                        prep_xT(t + 1, j)
                    if k == 3 and not last:
                        prep_q(t + 1, j)
                    raw_out(t, n)

            prep_xT(0, 0)
            prep_q(0, 0)
            prep_k(0, 0)
            prep_xT(0, 1)
            prep_q(0, 1)
            exps(0, 0)
            turn_act(0, True, False)
            with act.Fori(1, TURNS - 1) as t:
                turn_act(t, False, False)
            turn_act(TURNS - 1, False, True)
            context_out(G - 1)

            act.wait_ge(s_w2, 16 * n_expert_weights)
            act.wait_ge(s_var, 2)
            fn(tmp_b[:, :], tmp_a[:, :], ACT.Sqrt).then_inc(s_std, 1)

            def quad_act(q, b):
                act.wait_ge(s_zT, q + 1)
                wait_from_one(act, s_h, q * (E * CH) - E * CH)
                fn(xnT[:, b, :], P[:, 5, :], ACT.Identity, bias=beta_col[:, 0:1], scale=gamma_col[:, 0:1]).then_inc(s_xn, 1)
                act.wait_ge(s_gap, q + 1)
                fn(tanh_gap[:, :], gap[:, :], ACT.Tanh, scale=0.5).then_inc(s_tanh, 1)
                act.wait_ge(s_wfT, q + 1)
                wait_from_one(act, s_b2, q)
                fn(w_fullT[:, :, :].rearrange("e k n -> e (k n)"), P[0:E, 6, :], ACT.Identity).then_inc(s_wfTe, 1)
                for e in range(E):
                    wait_from_one(act, s_y, q * E + (e - 1))
                    for c in range(CH):
                        act.wait_ge(s_h, q * (E * CH) + (e * CH + c + 1))
                        fn(hid[:, e % 2, c, :], P[:, (e * CH + c) % 2, :], ACT.Gelu, bias=b1_col[:, e, c:c + 1]).then_inc(s_g, 1)

            quad_act(0, 0)
            quad_act(1, 1)
            with act.Fori(1, QUADS // 2) as p:
                quad_act(p * 2, 0)
                quad_act(p * 2 + 1, 1)

        @block.vector
        def _(dve):
            v = nc.vector
            chain = [0]

            def then(ins):
                chain[0] += 1
                ins.then_inc(s_ln, 1)
                dve.wait_ge(s_ln, chain[0])

            v.memset(ones_row[:, :], 1.0).then_inc(s_ones, 1)
            for j in range(2):
                v.memset(k_diag[:, j].rearrange("p k h m -> p (k h m)"), 0.0).then_inc(s_kd_zero, 1)
            then(v.memset(v_slots[:, :, :, :, :].rearrange("p b k h s -> p (b k h s)"), 0.0))
            v.memset(v_slots[:, :, :, :, HD:HD + 1].rearrange("p b k h s -> p (b k h) s"), 1.0).then_inc(s_v_ones, 1)

            def mean_and_m2():
                me, mo = stats[:, :, 1], stats[:, :, 4]
                then(v.tensor_tensor(tmp_b[:, :], me, mo, ALU.subtract))
                then(v.tensor_scalar(tmp_b[:, :], tmp_b[:, :], 0.5, None, ALU.mult))
                then(v.tensor_tensor(tmp_b[:, :], tmp_b[:, :], tmp_b[:, :], ALU.mult))
                then(v.tensor_tensor(mean[:, :], me, mo, ALU.add))
                then(v.tensor_scalar(mean[:, :], mean[:, :], 0.5, None, ALU.mult))
                then(v.tensor_tensor(tmp_a[:, :], stats[:, :, 2], stats[:, :, 5], ALU.add))
                then(v.scalar_tensor_tensor(out=tmp_a[:, :], in0=tmp_a[:, :], scalar=1.0 / D, in1=tmp_b[:, :],
                                            op0=ALU.mult, op1=ALU.add))

            for t in range(TURNS):
                dve.wait_ge(s_x[t], 16)
                for g in range(t * TURN, (t + 1) * TURN):
                    last = v.bn_stats(stats[:, g, :], X[:, g, :])
            last.then_inc(s_stat, 1)
            dve.wait_ge(s_stat, 1)
            mean_and_m2()
            v.tensor_scalar(tmp_a[:, :], tmp_a[:, :], EPS, None, ALU.add).then_inc(s_var, 1)
            dve.wait_ge(s_w1, 16 * n_attn_weights)
            v.tensor_copy(bv_wide[:, :], bv_col[:, 0:1].to_broadcast([128, 128])).then_inc(s_bvw, 1)
            dve.wait_ge(s_std, 1)
            v.reciprocal(rstd[:, :], tmp_b[:, :]).then_inc(s_rstd, 1)
            dve.wait_ge(s_ab_mm, 1)
            v.tensor_copy(attn_bias[:, :], P[:, P_CTX, 0:D]).then_inc(s_ab, 1)

            def mask(t, j):
                dve.wait_ge(s_adj[j], t * 16 + 16)
                wait_from_one(dve, s_sc, t * 16 + (8 * j - 8))
                v.tensor_scalar(mask_bias[:, j], adj_raw[:, j], 0.0, MASKED, ALU.is_equal, ALU.mult).then_inc(s_mask, 1)

            def v_out(t, j):
                dve.wait_ge(s_vmm, t * 2 + j + 1)
                wait_from_one(dve, s_pv, t * TURN + (QUAD * j - QUAD))
                v.tensor_copy(v_slots[:, j, :, :, 0:HD].rearrange("p k h d -> p (k h) d"),
                              P[:, P_PREP, :].rearrange("p (a d) -> p a d", d=HD)).then_inc(s_v, 1)

            def score_banks(n):
                first = P_SCORES + 2 * (n % 2)
                return P[:, first:first + 2, :].rearrange("p b (h m) -> p (b h) m", h=HALF)

            def maxima(t, n):
                dve.wait_ge(s_sc, (t * TURN + n) * 2 + 2)
                if n == 0:
                    wait_from_one(dve, s_edge, t)
                v.reduce_max(row_max[:, n, :], score_banks(n), AX).then_inc(s_max, 1)

            def less_max(t, n):
                dve.wait_ge(s_max, t * TURN + n + 1)
                wait_from_one(dve, s_pT, (t * TURN + n) * 2 - 2)
                m = row_max[:, n, :].unsqueeze(2).to_broadcast([128, HEADS, N])
                v.tensor_tensor(probs[:, n % 2], score_banks(n), m, ALU.subtract).then_inc(s_sub, 1)

            def normalise(g):
                dve.wait_ge(s_back, g + 1)
                back = P[:, P_CTX, 0:256].rearrange("p (h s) -> p h s", s=SLOT)
                v.reciprocal(rden[:, :], back[:, :, HD]).then_inc(s_rden, 1)
                dve.wait_ge(s_rden, g + 1)
                v.tensor_tensor(ctxn[:, :, :], back[:, :, 0:HD], rden[:, :].unsqueeze(2).to_broadcast([128, HEADS, HD]),
                                ALU.mult).then_inc(s_norm, 1)

            def residual(t, n):
                g = t * TURN + n
                dve.wait_ge(s_wo, g + 1)
                dve.wait_ge(s_xc, t * 2 + n // QUAD + 1)
                xg = X[:, bass.ds(g, 1), :].rearrange("p a d -> p (a d)")
                v.tensor_tensor(xg, P[:, P_CTX, 0:D], xg, ALU.add).then_inc(s_res, 1)
                dve.wait_ge(s_res, g + 1)
                v.bn_stats(stats[:, bass.ds(g, 1), :].rearrange("p a d -> p (a d)"), xg).then_inc(s_st2, 1)

            def flag_rows(t):
                dve.wait_ge(s_max, t * TURN + TURN)
                v.tensor_scalar(no_edge[:, bass.ds(t * TURN, TURN)], row_max[:, :, 0], EMPTY_ROW, HUGE, ALU.is_le,
                                ALU.mult).then_inc(s_edge, 1)

            def turn_dve(t, first, last):
                for n in range(TURN):
                    if n == TURN - 1:
                        flag_rows(t)
                    prev = not (first and n == 0)
                    more = not (last and n + 1 >= TURN)
                    nxt = (t + (n + 1) // TURN, (n + 1) % TURN)
                    j, k = n // QUAD, n % QUAD
                    if more:
                        maxima(*nxt)
                    if prev:
                        normalise(t * TURN + (n - 1))
                    if more:
                        less_max(*nxt)
                    if k == 0 and not (last and j == 1):
                        mask(t + (j + 1) // 2, (j + 1) % 2)
                    if prev:
                        residual(*((t, n - 1) if n else (t - 1, TURN - 1)))
                    if k == 1 and not (last and j == 1):
                        v_out(t + (j + 1) // 2, (j + 1) % 2)

            mask(0, 0)
            dve.wait_ge(s_v_ones, 1)
            v_out(0, 0)
            maxima(0, 0)
            less_max(0, 0)
            turn_dve(0, True, False)
            with dve.Fori(1, TURNS - 1) as t:
                turn_dve(t, False, False)
            turn_dve(TURNS - 1, False, True)
            normalise(G - 1)
            residual(TURNS - 1, TURN - 1)

            dve.wait_ge(s_st2, G)
            dve.wait_ge(s_edge, TURNS)
            v.tensor_scalar(no_edge[:, :], no_edge[:, :], HUGE, 0.0, ALU.mult, ALU.mult).then_inc(s_nan, 1)
            dve.wait_ge(s_nan, 1)
            mean_and_m2()
            v.tensor_scalar(tmp_a[:, :], tmp_a[:, :], 1.0 + EPS, EPS * EPS, ALU.mult, ALU.add).then_inc(s_var, 1)
            dve.wait_ge(s_std, 2)
            v.reciprocal(rstd[:, :], tmp_b[:, :]).then_inc(s_rstd2, 1)
            dve.wait_ge(s_rstd2, 1)

            def quad_dve(q, b, stored):
                wait_from_one(dve, s_zT, q)
                for k in range(QUAD):
                    g = q * QUAD + k
                    last = v.tensor_scalar(z[:, k, :], X[:, bass.ds(g, 1), :].rearrange("p a d -> p (a d)"),
                                           mean[:, bass.ds(g, 1)], rstd[:, bass.ds(g, 1)], ALU.subtract, ALU.mult)
                last.then_inc(s_z, 1)
                dve.wait_ge(s_lg, q + 1)
                v.tensor_copy(logit[:, :, :].rearrange("p k e -> p (k e)"), P[:, 6, 0:QUAD * E]).then_inc(s_l, 1)
                dve.wait_ge(s_rstd2, 1)
                dve.wait_ge(s_l, q + 1)
                for k in range(QUAD):
                    last = v.max(top[:, k, :], logit[:, k, :])
                last.then_inc(s_rt, 1)
                dve.wait_ge(s_rt, q * 6 + 1)
                v.tensor_tensor(gap[:, :], top[:, :, 0], top[:, :, 1], ALU.subtract).then_inc(s_gap, 1)
                for k in range(QUAD):
                    last = v.max_index(top_i[:, k, :], top[:, k, :], logit[:, k, :])
                last.then_inc(s_rt, 1)
                dve.wait_ge(s_rt, q * 6 + 2)
                v.tensor_copy(top_f[:, :, :], top_i[:, :, 0:2]).then_inc(s_rt, 1)
                dve.wait_ge(s_tanh, q + 1)
                v.scalar_tensor_tensor(out=gap[:, :], in0=tanh_gap[:, :], scalar=0.5, in1=no_edge[:, bass.ds(q * QUAD, QUAD)],
                                       op0=ALU.mult, op1=ALU.add).then_inc(s_rt, 1)
                dve.wait_ge(s_rt, q * 6 + 4)
                for i in range(2):
                    last = v.tensor_scalar(gates[:, :, i], gap[:, :], 1.0 - 2 * i, 0.5, ALU.mult, ALU.add)
                last.then_inc(s_rt, 1)
                dve.wait_ge(s_rt, q * 6 + 5)
                for i in range(2):
                    for k in range(QUAD):
                        last = v.tensor_scalar(pick[:, i, k, :], iota_e[:, :], top_f[:, k, i:i + 1], gates[:, k, i:i + 1],
                                               ALU.is_equal, ALU.mult)
                last.then_inc(s_rt, 1)
                dve.wait_ge(s_rt, q * 6 + 6)
                v.tensor_tensor(w_full[:, b], pick[:, 0], pick[:, 1], ALU.add).then_inc(s_wf, 1)
                dve.wait_ge(s_b2, q + 1)
                wait_from_one(dve, s_out[b], stored)
                for k in range(QUAD):
                    g = q * QUAD + k
                    last = v.tensor_tensor(acc[:, b, k, :], P[:, 7, k * D:(k + 1) * D],
                                           X[:, bass.ds(g, 1), :].rearrange("p a d -> p (a d)"), ALU.add)
                last.then_inc(s_acc0, 1)
                dve.wait_ge(s_acc0, q + 1)
                for e in range(E):
                    dve.wait_ge(s_y, q * E + e + 1)
                    for k in range(QUAD):
                        if e:
                            dve.wait_ge(s_acc, q * (E * QUAD) + ((e - 1) * QUAD + k + 1))
                        v.scalar_tensor_tensor(out=acc[:, b, k, :], in0=P[:, 3 + e % 2, k * D:(k + 1) * D],
                                               scalar=w_full[:, b, k, e:e + 1], in1=acc[:, b, k, :],
                                               op0=ALU.mult, op1=ALU.add).then_inc(s_acc, 1)

            quad_dve(0, 0, 0)
            quad_dve(1, 1, 0)
            with dve.Fori(1, QUADS // 2) as p:
                quad_dve(p * 2, 0, p * 16)
                quad_dve(p * 2 + 1, 1, p * 16)


_INS = ["x", "adj", "L0_gnn_Wq", "L0_gnn_bq", "L0_gnn_Wk", "L0_gnn_bk", "L0_gnn_Wv", "L0_gnn_bv", "L0_gnn_Wo",
        "L0_gnn_bo", "L0_ffn_gamma", "L0_ffn_beta", "L0_ffn_Wr", "L0_ffn_br", "L0_ffn_W1", "L0_ffn_b1", "L0_ffn_W2",
        "L0_ffn_b2"]


def kernel(**inputs):
    import numpy as _np
    import concourse.bacc as _bacc
    from concourse import mybir as _mybir
    from concourse.bass_utils import run_bass_kernel_spmd as _run

    nc = _bacc.Bacc("TRN2", target_bir_lowering=False, num_devices=1)
    arrays, args = {}, []
    for name in _INS:
        a = _np.ascontiguousarray(inputs[name])
        arrays[f"in_{name}_dram"] = a
        args.append(nc.dram_tensor(f"in_{name}_dram", a.shape, _mybir.dt.from_np(a.dtype), kind="ExternalInput").ap())
    out = nc.dram_tensor("out_0_dram", inputs["x"].shape, _mybir.dt.float32, kind="ExternalOutput").ap()
    build(nc, *args, out)
    r = _run(nc, [arrays], core_ids=[0])
    return r.results[0]["out_0_dram"]
```

```python
from contextlib import ExitStack

import concourse.bass as bass
from concourse import mybir

F32 = mybir.dt.float32
BF16 = mybir.dt.bfloat16
I32 = mybir.dt.int32
U32 = mybir.dt.uint32
ALU = mybir.AluOpType
ACT = mybir.ActivationFunctionType
AX = mybir.AxisListType.X

MASKED = -1.0e30
EMPTY_ROW = -5.0e29
HUGE = 3.0e38
EPS = 1e-05
HEADS = 8
RING = 4
SLOT = 32
QUAD = 4
TURN = 8


def wait_from_one(engine, semaphore, value):
    if isinstance(value, int) and value <= 0:
        return
    engine.wait_ge(semaphore, value)


def build(nc, x, adj, Wq, bq, Wk, bk, Wv, bv, Wo, bo, gamma, beta, Wr, br, W1, b1, W2, b2, out):
    G, N, D = x.shape
    E, _, HID = W1.shape
    HD = D // HEADS
    CH = HID // 128
    HALF = HEADS // 2
    TURNS = G // TURN
    QUADS = G // QUAD
    TOKENS = G * N
    ROW = D + 2
    REGION = TOKENS + 128
    TILES = (2 * TOKENS + E * 127) // 128
    PADS = E + TILES - 2 * TOKENS // 128
    SPARE = PADS - E
    TOKEN_STEP = 2 * 2 * QUAD * N
    EW = CH * 128 + CH * D + CH + D
    EW_W2, EW_B1, EW_B2 = CH * 128, CH * 128 + CH * D, CH * 128 + CH * D + CH
    table = nc.dram_tensor("table", [E * REGION + SPARE * 128, ROW], F32, kind="Internal").ap()
    results = nc.dram_tensor("results", [2 * TOKENS + PADS * 128, D], F32, kind="Internal").ap()
    assert N == 128 and D == 128 and W2.shape[2] == D and G % TURN == 0 and E == 8

    with ExitStack() as ctx:
        def sb(name, shape, dt=F32):
            return ctx.enter_context(nc.sbuf_tensor(name, shape, dt))

        def sem(name):
            return ctx.enter_context(nc.semaphore(name))

        X = sb("X", [128, G, D])
        ident = sb("ident", [128, 128])
        identb = sb("identb", [128, 128], BF16)
        ones_row = sb("ones_row", [1, 128])
        wq = sb("wq", [D, D])
        wk = sb("wk", [D, D])
        wv = sb("wv", [D, D])
        wo = sb("wo", [D, D])
        bq_col = sb("bq_col", [D, 1])
        bk_col = sb("bk_col", [D, 1])
        bv_col = sb("bv_col", [D, 1])
        bv_wide = sb("bv_wide", [D, 128])
        bo_row = sb("bo_row", [1, D])
        attn_bias = sb("attn_bias", [128, D])
        gamma_col = sb("gamma_col", [D, 1])
        beta_col = sb("beta_col", [D, 1])
        wr = sb("wr", [D, E])
        br_row = sb("br_row", [1, E])
        iota_e = sb("iota_e", [128, E])
        stats = sb("stats", [128, G, 6])
        mean = sb("mean", [128, G])
        rstd = sb("rstd", [128, G])
        tmp_a = sb("tmp_a", [128, G])
        tmp_b = sb("tmp_b", [128, G])
        stats2 = sb("stats2", [128, 2, QUAD, 6])
        mean2 = sb("mean2", [128, 2, QUAD])
        mean_sum = sb("mean_sum", [128, QUAD])
        mean_gap = sb("mean_gap", [128, QUAD])
        m2_sum = sb("m2_sum", [128, QUAD])
        var2 = sb("var2", [128, QUAD])
        ln_var = sb("ln_var", [128, QUAD])
        guess = sb("guess", [128, QUAD])
        newton = sb("newton", [128, QUAD])
        rstd2 = sb("rstd2", [128, 2, QUAD])
        adj_raw = sb("adj_raw", [128, 2, QUAD, N], I32)
        mask_bias = sb("mask_bias", [128, 2, QUAD, N], BF16)
        xhat = sb("xhat", [128, QUAD, D])
        xT = sb("xT", [D, QUAD * N])
        qT = sb("qT", [D, 2, QUAD * N])
        kT = sb("kT", [D, QUAD * N])
        k_diag = sb("k_diag", [D, 2, QUAD, HEADS, N])
        v_slots = sb("v_slots", [128, 2, QUAD, HEADS, SLOT])
        probs = sb("probs", [128, 2, HEADS, N])
        probsT = sb("probsT", [128, HEADS, N])
        row_max = sb("row_max", [128, TURN, HEADS])
        no_edge = sb("no_edge", [128, G])
        ctxT_raw = sb("ctxT_raw", [128, 2 * N])
        rden = sb("rden", [128, HEADS])
        ctxn = sb("ctxn", [128, HEADS, HD])
        ctxT = sb("ctxT", [D, N])
        token_row = sb("token_row", [128, 2, QUAD, ROW])
        token_step = sb("token_step", [128, QUAD])
        z_mid = sb("z_mid", [128, QUAD, D])
        xnT = sb("xnT", [D, QUAD * N])
        br_wide = sb("br_wide", [128, QUAD, E])
        logit = sb("logit", [128, QUAD, E])
        top = sb("top", [128, QUAD, E])
        top_i = sb("top_i", [128, QUAD, E], U32)
        top_f = sb("top_f", [128, QUAD, 2])
        gap = sb("gap", [128, QUAD])
        exp_gap = sb("exp_gap", [128, G])
        gates = sb("gates", [128, 2, G])
        pick = sb("pick", [128, 2, QUAD, E])
        picked = sb("picked", [128, QUAD, E], BF16)
        before = sb("before", [128, 128], BF16)
        all_ones = sb("all_ones", [128, 128], BF16)
        base = sb("base", [128, E])
        place = sb("place", [128, QUAD, E])
        placed = sb("placed", [128, 2, QUAD, E])
        place_f = sb("place_f", [128, 2, QUAD])
        place_i = sb("place_i", [128, 2, 2, QUAD], U32)
        pad_row = sb("pad_row", [128, PADS, ROW])
        part_f = sb("part_f", [128, 1])
        pad_i = sb("pad_i", [128, E], U32)
        region = sb("region", [128, E])
        count_i = sb("count_i", [128, E], I32)
        tiles_i = sb("tiles_i", [128, E], I32)
        tiles_of = sb("tiles_of", [128, E])
        tiles_upto = sb("tiles_upto", [128, E])
        skip = sb("skip", [128, E])
        tile_no = sb("tile_no", [128, TILES])
        tile_e = sb("tile_e", [128, TILES])
        tile_row = sb("tile_row", [128, TILES])
        tile_tmp = sb("tile_tmp", [128, 2, TILES])
        tile_e_i = sb("tile_e_i", [128, TILES], I32)
        tile_row_i = sb("tile_row_i", [128, TILES], I32)
        ew = sb("ew", [128, E, EW])
        tw = sb("tw", [128, RING, EW])
        t_row = sb("t_row", [128, RING, ROW])
        t_xnT = sb("t_xnT", [D, RING, 128])
        t_hid = sb("t_hid", [128, RING, CH, 128])
        t_y = sb("t_y", [128, RING, D])
        to_f = sb("to_f", [128, RING])
        to_i = sb("to_i", [128, RING], U32)
        both = sb("both", [128, RING, QUAD, 2 * D])

        P = ctx.enter_context(nc.psum_tensor("P", [128, 8, 512], F32))
        P_SCORES, P_T, P_PREP, P_CTX = 0, 4, 6, 7
        R_LOGIT, R_RANK, R_TOTAL = 256, 256 + QUAD * E, 256 + 2 * QUAD * E
        P_TT, P_TH, P_TY = 0, 2, 2 + 2 * CH

        block = ctx.enter_context(nc.Block())

        s_w1 = sem("s_attention_weights_loaded")
        s_w2 = sem("s_expert_weights_loaded")
        s_x = [sem(f"s_x_loaded_{t}") for t in range(TURNS)]
        s_ones = sem("s_ones")
        s_ident0 = sem("s_ident_zeroed")
        s_const = sem("s_constants")
        s_v_ones = sem("s_v_slots_preset")
        s_kd_zero = sem("s_k_diag_zeroed")
        s_stat = sem("s_stats1")
        s_ln = sem("s_ln_chain")
        s_var = sem("s_var_ready")
        s_std = sem("s_std_ready")
        s_rstd = sem("s_rstd_ready")
        s_ab_mm = sem("s_attn_bias_product")
        s_ab = sem("s_attn_bias")
        s_bvw = sem("s_bv_wide")
        s_adj = [sem(f"s_adj_loaded_{b}") for b in range(2)]
        s_mask = sem("s_mask_bias")
        s_centred = sem("s_x_less_mean")
        s_xhat = sem("s_xhat")
        s_xhatT = sem("s_xhatT")
        s_xT = sem("s_xT")
        s_qmm = sem("s_q_product")
        s_q = sem("s_qT")
        s_kmm = sem("s_k_product")
        s_k = sem("s_kT")
        s_kd = [sem(f"s_k_diag_{b}") for b in range(2)]
        s_vmm = sem("s_v_product")
        s_v = sem("s_v_slots")
        s_sc = sem("s_scores")
        s_max = sem("s_row_max")
        s_edge = sem("s_no_edge")
        s_nan = sem("s_nan_rows")
        s_sub = sem("s_scores_less_max")
        s_exp = sem("s_probs")
        s_pT = sem("s_probsT_psum")
        s_pTe = sem("s_probsT")
        s_pv = sem("s_context_product")
        s_cr = sem("s_ctxT_raw")
        s_back = sem("s_context_back")
        s_rden = sem("s_rden")
        s_norm = sem("s_ctxn")
        s_cT = sem("s_ctxT_psum")
        s_cTe = sem("s_ctxT")
        s_wo = sem("s_out_product")
        s_xc = sem("s_x_plus_bias")
        s_res = sem("s_residual")
        s_st2 = sem("s_stats2")
        s_br = sem("s_br_wide")
        s_ln2 = sem("s_second_norm_chain")
        s_var2 = sem("s_var2")
        s_lnv = sem("s_ln_var")
        s_guess = sem("s_rstd2_guess")
        s_rstd2 = sem("s_rstd2")
        s_zm = sem("s_z_mid")
        s_z = sem("s_z")
        s_zT = sem("s_zT")
        s_xn = sem("s_xnT")
        s_lg = sem("s_logits_product")
        s_logit = sem("s_logits")
        s_rt = sem("s_route_chain")
        s_gap = sem("s_gap")
        s_eg = sem("s_exp_gap")
        s_pick = sem("s_picked")
        s_rank = sem("s_ranks")
        s_pl = sem("s_place_chain")
        s_place = sem("s_places")
        s_token = sem("s_token_column")
        s_scat = [sem(f"s_rows_scattered_{b}") for b in range(2)]
        s_pad_set = sem("s_pad_rows_preset")
        s_spare = sem("s_spare_rows_stored")
        s_pad = sem("s_pad_places")
        s_pad_scat = sem("s_pads_scattered")
        s_tb = sem("s_tile_table_chain")
        s_tab = sem("s_tile_tables")
        s_load = [sem(f"s_tile_loaded_{b}") for b in range(RING)]
        s_tw = sem("s_tile_weights")
        s_to = sem("s_tile_destinations")
        s_tT = sem("s_tile_transposed")
        s_txn = sem("s_tile_xnT")
        s_th = sem("s_tile_hidden_product")
        s_tg = sem("s_tile_gelu")
        s_ty = sem("s_tile_product")
        s_y = [sem(f"s_tile_result_{b}") for b in range(RING)]
        s_ys = [sem(f"s_tile_scattered_{b}") for b in range(RING)]
        s_both = [sem(f"s_results_loaded_{b}") for b in range(RING)]
        s_gt = sem("s_gate_chain")
        s_add = sem("s_sum_chain")
        s_out = sem("s_out_stored")

        n_attn_weights, n_expert_weights = 9, 9

        def col(ap):
            return ap.rearrange("(p a) -> p a", a=1)

        def row(ap):
            return ap.rearrange("(a n) -> a n", a=1)

        adj_q = adj.rearrange("(q k) n m -> q n k m", k=QUAD)
        out_q = out.rearrange("(q k) n d -> q n k d", k=QUAD)

        def missing(t, c):
            return isinstance(t, int) and not 0 <= 2 * t + c < QUADS

        def upto(t, c, each=1, more=0):
            return t * (2 * each) + (c * each + more)

        def laps(t, c, each=1, more=0):
            return t * each + (c // 2 * each + more)

        def quad_of(t, c):
            return bass.ds(t * TURN + c * QUAD, QUAD)

        FULL_LAPS = TILES // RING

        def before_tile(lap, b, n):
            return lap + (b - n) // RING, (b - n) % RING

        def no_tile(lap, b):
            return isinstance(lap, int) and not 0 <= RING * lap + b < TILES

        def tile_slots(engine, slot, extra):
            for b in range(RING):
                slot(0, b)
            with engine.Fori(1, FULL_LAPS) as lap:
                for b in range(RING):
                    slot(lap, b)
            for i in range(FULL_LAPS * RING, TILES + extra):
                slot(i // RING, i % RING)

        @block.sync
        def _(sp):
            x_t = x.rearrange("(t g) n d -> t n g d", g=TURN)
            sp.dma_start(X[:, 0:TURN, :], x_t[0]).then_inc(s_x[0], 16)
            sp.dma_start(adj_raw[:, 0], adj_q[0]).then_inc(s_adj[0], 16)
            sp.dma_start(adj_raw[:, 1], adj_q[1]).then_inc(s_adj[1], 16)
            for dst, src in ((wq[:, :], Wq), (wk[:, :], Wk), (wv[:, :], Wv), (wo[:, :], Wo),
                             (bq_col[:, :], col(bq)), (bk_col[:, :], col(bk)), (bv_col[:, :], col(bv)),
                             (bo_row[:, :], row(bo)), (br_row[:, :], row(br))):
                sp.dma_start(dst, src).then_inc(s_w1, 16)
            for t in range(1, TURNS):
                sp.dma_start(X[:, t * TURN:(t + 1) * TURN, :], x_t[t]).then_inc(s_x[t], 16)
            for dst, src in ((gamma_col[:, :], col(gamma)), (beta_col[:, :], col(beta)), (wr[:, :], Wr),
                             (ew[:, :, 0:HID], W1.rearrange("e d h -> d e h")),
                             (ew[:, :, EW_B2:EW_B2 + D], b2.unsqueeze(0).to_broadcast([128, E, D]))):
                sp.dma_start(dst, src).then_inc(s_w2, 16)
            for c in range(CH):
                sp.dma_start(ew[:, :, EW_W2 + c * D:EW_W2 + (c + 1) * D],
                             W2[:, c * 128:(c + 1) * 128, :].rearrange("e p d -> p e d")).then_inc(s_w2, 16)
                sp.dma_start(ew[:, :, EW_B1 + c:EW_B1 + c + 1], b1[:, c * 128:(c + 1) * 128].rearrange("e (p a) -> p e a", a=1),
                             allow_slow_non_contiguous=True).then_inc(s_w2, 16)
            sp.wait_ge(s_pad_set, 3)
            sp.dma_start(table[E * REGION:E * REGION + SPARE * 128, :].rearrange("(i p) c -> p i c", p=128),
                         pad_row[:, E:PADS, :]).then_inc(s_spare, 16)

            def spread_k(turn, j):
                sp.wait_ge(s_kd_zero, 2)
                sp.wait_ge(s_k, turn * 2 + j + 1)
                for h in range(HEADS):
                    rows = slice(h * HD, (h + 1) * HD)
                    sp.dma_start(k_diag[rows, j, :, h, :], kT[rows, :].rearrange("p (k n) -> p k n", k=QUAD)).then_inc(s_kd[j], 16)

            sp.wait_ge(s_kd_zero, 2)
            spread_k(0, 0)

            def turn_sp(t, last):
                for j in range(2):
                    if not (last and j == 1):
                        spread_k(t + (j + 1) // 2, (j + 1) % 2)
                    if not last:
                        sp.wait_ge(s_kd_zero, 2)
                        sp.wait_ge(s_mask, t * 2 + j + 1)
                        sp.dma_start(adj_raw[:, j], adj_q[t * 2 + (j + 2)]).then_inc(s_adj[j], 16)

            turn_sp(0, False)
            with sp.Fori(1, TURNS - 1) as t:
                turn_sp(t, False)
            turn_sp(TURNS - 1, True)

            for r in range(2):
                sp.wait_ge(s_scat[r], 16 * 2 * QUAD * (QUADS // 2))
            sp.wait_ge(s_spare, 16)
            sp.wait_ge(s_pad_scat, 16 * E)
            sp.wait_ge(s_tab, 1)

            def load_tile(lap, b):
                first = sp.value_load(tile_row_i[0:1, bass.ds(lap * RING + b, 1)], min_val=0,
                                      max_val=E * REGION + SPARE * 128 - 128)
                wait_from_one(sp, s_tT, lap * RING + (b - RING + 1))
                wait_from_one(sp, s_to, lap * RING + (b - RING + 1))
                sp.dma_start(t_row[:, b, :], table[bass.ds(first, 128), :]).then_inc(s_load[b], 16)

            tile_slots(sp, load_tile, 0)

            for b in range(RING):
                sp.wait_ge(s_ys[b], 16 * len(range(b, TILES, RING)))
            pairs = results[0:2 * TOKENS, :].rearrange("(q k n i) d -> q n k (i d)", k=QUAD, n=N, i=2)

            def load_both(lap, b):
                sp.wait_ge(s_spare, 16)
                wait_from_one(sp, s_add, lap * (RING * 2 * QUAD) + (b - RING + 1) * 2 * QUAD)
                sp.dma_start(both[:, b], pairs[lap * RING + b]).then_inc(s_both[b], 16)

            for b in range(RING):
                load_both(0, b)
            with sp.Fori(1, QUADS // RING) as lap:
                for b in range(RING):
                    load_both(lap, b)

        @block.gpsimd
        def _(pool):
            nc.gpsimd.memset(ident[:, :], 0.0).then_inc(s_ident0, 1)
            nc.gpsimd.memset(identb[:, :], 0.0).then_inc(s_ident0, 1)
            pool.wait_ge(s_ident0, 2)
            for m in (ident, identb):
                nc.gpsimd.affine_select(out=m[:, :], in_=m[:, :], compare_op=ALU.not_equal, fill=1.0, base=0,
                                        pattern=[[-1, 128]], channel_multiplier=1).then_inc(s_const, 1)
            nc.gpsimd.iota(iota_e[:, :], pattern=[[1, E]], base=0, channel_multiplier=0,
                           allow_small_or_imprecise_dtypes=True).then_inc(s_const, 1)
            all_rows = pad_row[:, :, :].rearrange("p i c -> p (i c)")
            nc.gpsimd.memset(all_rows, 0.0).then_inc(s_pad_set, 1)
            nc.gpsimd.memset(all_ones[:, :], 1.0).then_inc(s_const, 1)
            nc.gpsimd.memset(token_step[:, :], float(TOKEN_STEP)).then_inc(s_const, 1)
            nc.gpsimd.iota(region[:, :], pattern=[[REGION, E]], base=0, channel_multiplier=0,
                           allow_small_or_imprecise_dtypes=True).then_inc(s_const, 1)
            nc.gpsimd.iota(part_f[:, :], pattern=[[0, 1]], base=0, channel_multiplier=1,
                           allow_small_or_imprecise_dtypes=True).then_inc(s_const, 1)
            nc.gpsimd.iota(tile_no[:, :], pattern=[[1, TILES]], base=0, channel_multiplier=0,
                           allow_small_or_imprecise_dtypes=True).then_inc(s_const, 1)
            for r in range(2):
                nc.gpsimd.iota(token_row[:, r, :, D], pattern=[[2 * N, QUAD]], base=r * QUAD * N * 2 - TOKEN_STEP,
                               channel_multiplier=2, allow_small_or_imprecise_dtypes=True).then_inc(s_const, 1)
            pool.wait_ge(s_const, 10)
            nc.gpsimd.affine_select(out=before[:, :], in_=all_ones[:, :], compare_op=ALU.is_gt, fill=0.0, base=0,
                                    pattern=[[1, 128]], channel_multiplier=-1).then_inc(s_const, 1)
            pool.wait_ge(s_pad_set, 1)
            nc.gpsimd.iota(pad_row[:, :, D], pattern=[[128, PADS]], base=2 * TOKENS - 1, channel_multiplier=1,
                           allow_small_or_imprecise_dtypes=True).then_inc(s_pad_set, 1)
            nc.gpsimd.memset(pad_row[:, :, D + 1], -1.0).then_inc(s_pad_set, 1)

            def normalise(t, j):
                quad = bass.ds(t * TURN + QUAD * j, QUAD)
                wide = [128, QUAD, D]
                pool.wait_ge(s_rstd, 1)
                wait_from_one(pool, s_xhatT, t * 2 + j)
                nc.gpsimd.tensor_tensor(xhat[:, :, :], X[:, quad, :], mean[:, quad].unsqueeze(2).to_broadcast(wide),
                                        ALU.subtract).then_inc(s_centred, 1)
                pool.wait_ge(s_rstd, 1)
                pool.wait_ge(s_centred, t * 2 + j + 1)
                nc.gpsimd.tensor_tensor(xhat[:, :, :], xhat[:, :, :], rstd[:, quad].unsqueeze(2).to_broadcast(wide),
                                        ALU.mult).then_inc(s_xhat, 1)
                pool.wait_ge(s_ab, 1)
                nc.gpsimd.tensor_tensor(X[:, quad, :], X[:, quad, :], attn_bias[:, :].unsqueeze(1).to_broadcast(wide),
                                        ALU.add).then_inc(s_xc, 1)

            def normalise2(t, c):
                if missing(t, c):
                    return
                r, wide = c % 2, [128, QUAD, D]
                pool.wait_ge(s_const, 11)
                pool.wait_ge(s_rstd2, upto(t, c, 1, 1))
                nc.gpsimd.tensor_tensor(z_mid[:, :, :], X[:, quad_of(t, c), :], mean2[:, r, :].unsqueeze(2).to_broadcast(wide),
                                        ALU.subtract).then_inc(s_zm, 1)
                pool.wait_ge(s_zm, upto(t, c, 1, 1))
                wait_from_one(pool, s_scat[r], laps(t, c, 16 * 2 * QUAD))
                nc.gpsimd.tensor_tensor(token_row[:, r, :, 0:D], z_mid[:, :, :], rstd2[:, r, :].unsqueeze(2).to_broadcast(wide),
                                        ALU.mult).then_inc(s_z, 1)

            def scatter(t, c):
                if missing(t, c):
                    return
                r = c % 2
                pool.wait_ge(s_place, upto(t, c, 1, 1))
                nc.gpsimd.tensor_tensor(token_row[:, r, :, D], token_row[:, r, :, D], token_step[:, :], ALU.add).then_inc(s_token, 1)
                pool.wait_ge(s_const, 11)
                pool.wait_ge(s_token, upto(t, c, 1, 1))
                for i in range(2):
                    for k in range(QUAD):
                        nc.gpsimd.indirect_dma_start(
                            out=table, out_offset=bass.IndirectOffsetOnAxis(ap=place_i[:, r, i, k:k + 1], axis=0),
                            in_=token_row[:, r, k, :], in_offset=None).then_inc(s_scat[r], 16)

            normalise(0, 0)
            normalise(0, 1)

            def turn_pool(t, last):
                for j in range(2):
                    if not last:
                        normalise(t + 1, j)
                    scatter(t, j - 3)
                    normalise2(t, j - 1)

            turn_pool(0, False)
            turn_pool(1, False)
            with pool.Fori(2, TURNS - 1) as t:
                turn_pool(t, False)
            turn_pool(TURNS - 1, True)
            for c in range(3):
                scatter(TURNS, c - 3)
                normalise2(TURNS, c - 1)
            pool.wait_ge(s_pad, 1)
            pool.wait_ge(s_pad_set, 3)
            for e in range(E):
                nc.gpsimd.indirect_dma_start(out=table, out_offset=bass.IndirectOffsetOnAxis(ap=pad_i[:, e:e + 1], axis=0),
                                             in_=pad_row[:, e, :], in_offset=None).then_inc(s_pad_scat, 16)

            def scatter_tile(laps_done, b):
                pool.wait_ge(s_const, 11)
                pool.wait_ge(s_y[b], laps_done)
                nc.gpsimd.indirect_dma_start(out=results, out_offset=bass.IndirectOffsetOnAxis(ap=to_i[:, b:b + 1], axis=0),
                                             in_=t_y[:, b, :], in_offset=None).then_inc(s_ys[b], 16)

            for b in range(RING):
                scatter_tile(1, b)
            with pool.Fori(2, FULL_LAPS + 1) as laps_done:
                for b in range(RING):
                    scatter_tile(laps_done, b)
            for b in range(TILES % RING):
                scatter_tile(FULL_LAPS + 1, b)

        @block.tensor
        def _(pe):
            mm = nc.tensor.matmul

            pe.wait_ge(s_w1, 16 * n_attn_weights)
            pe.wait_ge(s_bvw, 1)
            pe.wait_ge(s_ones, 1)
            pe.wait_ge(s_const, 3)
            mm(P[:, P_CTX, 0:D], bv_wide[:, :], wo[:, :], start=True, stop=False)
            mm(P[:, P_CTX, 0:D], ones_row[:, :], bo_row[:, :], start=False, stop=True)
            mm(P[:, P_CTX, R_LOGIT:R_RANK].rearrange("p (k e) -> p k e", e=E), ones_row[:, :],
               br_row[:, :].unsqueeze(1).to_broadcast([1, QUAD, E]), start=True, stop=True).then_inc(s_ab_mm, 1)

            def prep_xT(t, j):
                pe.wait_ge(s_xhat, t * 2 + j + 1)
                wait_from_one(pe, s_v, t * 2 + j)
                wait_from_one(pe, s_xn, t * 2 + (j - 3))
                for k in range(QUAD):
                    last = nc.tensor.transpose(P[:, P_PREP, k * N:(k + 1) * N], xhat[:, k, :], ident[:, :])
                last.then_inc(s_xhatT, 1)

            def prep_q(t, j):
                pe.wait_ge(s_xT, t * 2 + j + 1)
                mm(P[:, P_PREP, :], wq[:, :], xT[:, :], start=True, stop=True).then_inc(s_qmm, 1)

            def prep_k(t, j):
                pe.wait_ge(s_q, t * 2 + j + 1)
                mm(P[:, P_PREP, :], wk[:, :], xT[:, :], start=True, stop=True).then_inc(s_kmm, 1)

            def prep_v(t, j):
                pe.wait_ge(s_k, t * 2 + j + 1)
                for k in range(QUAD):
                    last = mm(P[:, P_PREP, k * N:(k + 1) * N], xT[:, k * N:(k + 1) * N], wv[:, :], start=True, stop=True)
                last.then_inc(s_vmm, 1)

            def scores(t, n, half):
                t, n = t + n // TURN, n % TURN
                j, k = n // QUAD, n % QUAD
                bank = P_SCORES + 2 * (n % 2) + half
                if half == 0:
                    wait_from_one(pe, s_sub, t * TURN + (n - 1))
                    pe.wait_ge(s_mask, t * 2 + j + 1)
                    pe.wait_ge(s_q, t * 2 + j + 1)
                    pe.wait_ge(s_kd[j], t * (16 * HEADS) + 16 * HEADS)
                bias = mask_bias[:, j, k, :].unsqueeze(1).to_broadcast([128, HALF, N])
                mm(P[:, bank, :].rearrange("p (h m) -> p h m", h=HALF), identb[:, :], bias, start=True, stop=False)
                mm(P[:, bank, :], qT[:, j, k * N:(k + 1) * N],
                   k_diag[:, j, k, half * HALF:(half + 1) * HALF, :].rearrange("p h m -> p (h m)"),
                   start=False, stop=True).then_inc(s_sc, 1)

            def turn_probs(t, n):
                pe.wait_ge(s_exp, t * TURN + n + 1)
                for half in range(2):
                    wait_from_one(pe, s_pTe, (t * TURN + n) * 2 + (half - 1))
                    for h in range(HALF):
                        last = nc.tensor.transpose(P[:, P_T + half, h * N:(h + 1) * N], probs[:, n % 2, half * HALF + h, :], ident[:, :])
                    last.then_inc(s_pT, 1)

            def context(t, n):
                pe.wait_ge(s_pTe, (t * TURN + n) * 2 + 2)
                pe.wait_ge(s_v, t * 2 + n // QUAD + 1)
                wait_from_one(pe, s_res, t * TURN + n)
                j, k = n // QUAD, n % QUAD
                if k == 0 and not missing(t, j - 3):
                    pe.wait_ge(s_logit, upto(t, j - 3, 1, 1))
                if k == 1:
                    ranks(t, j - 3)
                if k == 2 and not missing(t, j - 3):
                    pe.wait_ge(s_pl, upto(t, j - 3, 4, 2))
                if k == 3:
                    logits(t, j - 2)
                for h in range(HEADS):
                    slot, group = h % HALF, h // HALF
                    last = mm(P[slot * SLOT:(slot + 1) * SLOT, P_CTX, group * N:(group + 1) * N],
                              v_slots[:, n // QUAD, n % QUAD, h, :], probsT[:, h, :], start=True, stop=True,
                              tile_position=(0, slot * SLOT))
                last.then_inc(s_pv, 1)

            def context_back(g):
                pe.wait_ge(s_cr, g + 1)
                for group in range(2):
                    last = nc.tensor.transpose(P[:, P_CTX, group * 128:(group + 1) * 128], ctxT_raw[:, group * N:(group + 1) * N], ident[:, :])
                last.then_inc(s_back, 1)

            def context_turn(g):
                pe.wait_ge(s_norm, g + 1)
                nc.tensor.transpose(P[:, P_CTX, 0:N], ctxn[:, :, :].rearrange("p h d -> p (h d)"), ident[:, :]).then_inc(s_cT, 1)

            def project(g):
                pe.wait_ge(s_cTe, g + 1)
                mm(P[:, P_CTX, 0:D], ctxT[:, :], wo[:, :], start=True, stop=True).then_inc(s_wo, 1)

            def z_transposed(t, c):
                if missing(t, c):
                    return
                pe.wait_ge(s_z, upto(t, c, 1, 1))
                pe.wait_ge(s_v, upto(t, c, 1, 4) if not isinstance(t, int) else min(upto(t, c, 1, 4), QUADS))
                wait_from_one(pe, s_xn, upto(t, c))
                for k in range(QUAD):
                    last = nc.tensor.transpose(P[:, P_PREP, k * N:(k + 1) * N], token_row[:, c % 2, k, 0:D], ident[:, :])
                last.then_inc(s_zT, 1)

            def logits(t, c):
                if missing(t, c):
                    return
                pe.wait_ge(s_w2, 16 * n_expert_weights)
                pe.wait_ge(s_br, 1)
                pe.wait_ge(s_xn, upto(t, c, 1, 1))
                wait_from_one(pe, s_pl, upto(t, c, 4, -2))
                for k in range(QUAD):
                    last = mm(P[:, P_CTX, R_LOGIT + k * E:R_LOGIT + (k + 1) * E], xnT[:, k * N:(k + 1) * N], wr[:, :],
                              start=True, stop=True)
                last.then_inc(s_lg, 1)

            def ranks(t, c):
                if missing(t, c):
                    return
                pe.wait_ge(s_const, 11)
                pe.wait_ge(s_pick, upto(t, c, 1, 1))
                wait_from_one(pe, s_place, upto(t, c))
                flat = picked[:, :, :].rearrange("p k e -> p (k e)")
                mm(P[:, P_CTX, R_RANK:R_TOTAL], before[:, :], flat, start=True, stop=False, skip_group_check=True)
                for k in range(1, QUAD):
                    mm(P[:, P_CTX, R_RANK + k * E:R_TOTAL], all_ones[:, :], flat[:, 0:(QUAD - k) * E], start=False,
                       stop=(k == QUAD - 1), skip_group_check=True)
                for k in range(QUAD):
                    last = mm(P[:, P_CTX, R_TOTAL:R_TOTAL + E], all_ones[:, :], flat[:, k * E:(k + 1) * E], start=(k == 0),
                              stop=(k == QUAD - 1), skip_group_check=True)
                last.then_inc(s_rank, 1)

            def turn_pe(t, first, last):
                for n in range(TURN):
                    prev = not (first and n == 0)
                    more = not (last and n + 2 >= TURN)
                    turn_probs(t, n)
                    if prev:
                        context_back(t * TURN + (n - 1))
                    if more:
                        scores(t, n + 2, 0)
                    if n % QUAD == 2:
                        z_transposed(t, n // QUAD - 2)
                    if prev:
                        context_turn(t * TURN + (n - 1))
                    if more:
                        scores(t, n + 2, 1)
                    if prev:
                        project(t * TURN + (n - 1))
                    j, k = n // QUAD, n % QUAD
                    one, two = (t + (j + 1) // 2, (j + 1) % 2), (t + 1, j)
                    if k == 0 and not (last and j == 1):
                        prep_k(*one)
                    if k == 1 and not (last and j == 1):
                        prep_v(*one)
                    if k == 2 and not last:
                        prep_xT(*two)
                    if k == 3 and not last:
                        prep_q(*two)
                    context(t, n)

            prep_xT(0, 0)
            prep_q(0, 0)
            prep_k(0, 0)
            prep_v(0, 0)
            prep_xT(0, 1)
            prep_q(0, 1)
            for n in range(2):
                for half in range(2):
                    scores(0, n, half)
            turn_pe(0, True, False)
            turn_pe(1, False, False)
            with pe.Fori(2, TURNS - 1) as t:
                turn_pe(t, False, False)
            turn_pe(TURNS - 1, False, True)
            context_back(G - 1)
            context_turn(G - 1)
            project(G - 1)

            for c in range(3):
                ranks(TURNS, c - 3)
                z_transposed(TURNS, c - 2)
                logits(TURNS, c - 2)

            pe.wait_ge(s_res, G)
            pe.wait_ge(s_place, QUADS)

            def tile_transposed(lap, b):
                pe.wait_ge(s_load[b], lap * 16 + 16)
                wait_from_one(pe, s_txn, lap * RING + (b - 1))
                nc.tensor.transpose(P[:, P_TT + b % 2, 0:128], t_row[:, b, 0:D], ident[:, :]).then_inc(s_tT, 1)

            def tile_hidden(lap, b):
                pe.wait_ge(s_txn, lap * RING + (b + 1))
                pe.wait_ge(s_tw, lap * RING + (b + 1))
                wait_from_one(pe, s_tg, lap * RING + (b - 1))
                for c in range(CH):
                    mm(P[:, P_TH + b % 2 * CH + c, 0:128], tw[:, b, c * 128:(c + 1) * 128], t_xnT[:, b, :],
                       start=True, stop=True).then_inc(s_th, 1)

            def tile_result(lap, b):
                pe.wait_ge(s_tg, lap * RING + (b + 1))
                two = before_tile(lap, b, 2)
                wait_from_one(pe, s_y[two[1]], two[0] + 1)
                for c in range(CH):
                    last = mm(P[:, P_TY + b % 2, 0:D], t_hid[:, b, c, :], tw[:, b, EW_W2 + c * D:EW_W2 + (c + 1) * D],
                              start=(c == 0), stop=(c == CH - 1))
                last.then_inc(s_ty, 1)

            def slot_pe(lap, b):
                for step, lag in ((tile_transposed, 0), (tile_hidden, 1), (tile_result, 3)):
                    tile = before_tile(lap, b, lag)
                    if not no_tile(*tile):
                        step(*tile)

            tile_slots(pe, slot_pe, 3)

        @block.scalar
        def _(act):
            fn = nc.scalar.activation
            act.wait_ge(s_w1, 16 * n_attn_weights)
            act.wait_ge(s_var, 1)
            fn(tmp_b[:, :], tmp_a[:, :], ACT.Sqrt).then_inc(s_std, 1)

            def prep_xT(t, j):
                act.wait_ge(s_xhatT, t * 2 + j + 1)
                wait_from_one(act, s_vmm, t * 2 + j)
                fn(xT[:, :], P[:, P_PREP, :], ACT.Identity).then_inc(s_xT, 1)

            def prep_q(t, j):
                act.wait_ge(s_qmm, t * 2 + j + 1)
                fn(qT[:, j, :], P[:, P_PREP, :], ACT.Identity, bias=bq_col[:, 0:1]).then_inc(s_q, 1)

            def prep_k(t, j):
                act.wait_ge(s_kmm, t * 2 + j + 1)
                if not (isinstance(t, int) and t == 0 and j == 0):
                    act.wait_ge(s_kd[1 - j], (t + (j - 1)) * (16 * HEADS) + 16 * HEADS if j == 0 else t * (16 * HEADS) + 16 * HEADS)
                fn(kT[:, :], P[:, P_PREP, :], ACT.Identity, bias=bk_col[:, 0:1]).then_inc(s_k, 1)

            def exps(t, n):
                act.wait_ge(s_sub, t * TURN + n + 1)
                p = probs[:, n % 2].rearrange("p h m -> p (h m)")
                fn(p, p, ACT.Exp, scale=float(HD) ** -0.5).then_inc(s_exp, 1)

            def probs_out(t, n):
                wait_from_one(act, s_pv, t * TURN + n)
                for half in range(2):
                    act.wait_ge(s_pT, (t * TURN + n) * 2 + half + 1)
                    fn(probsT[:, half * HALF:(half + 1) * HALF, :].rearrange("p h m -> p (h m)"), P[:, P_T + half, :], ACT.Identity).then_inc(s_pTe, 1)

            def context_out(g):
                act.wait_ge(s_cT, g + 1)
                fn(ctxT[:, :], P[:, P_CTX, 0:N], ACT.Identity).then_inc(s_cTe, 1)

            def raw_out(t, n):
                act.wait_ge(s_pv, t * TURN + n + 1)
                fn(ctxT_raw[:, :], P[:, P_CTX, 0:2 * N], ACT.Identity).then_inc(s_cr, 1)

            def log_std(t, c):
                if missing(t, c):
                    return
                act.wait_ge(s_var2, upto(t, c, 1, 1))
                fn(ln_var[:, :], var2[:, :], ACT.Ln).then_inc(s_lnv, 1)
                act.wait_ge(s_lnv, upto(t, c, 1, 1))
                fn(guess[:, :], ln_var[:, :], ACT.Exp, scale=-0.5).then_inc(s_guess, 1)

            def exp_of_gap(t, c):
                if missing(t, c):
                    return
                act.wait_ge(s_gap, upto(t, c, 1, 1))
                fn(exp_gap[:, quad_of(t, c)], gap[:, :], ACT.Exp).then_inc(s_eg, 1)

            def xn_out(t, c):
                if missing(t, c):
                    return
                act.wait_ge(s_w2, 16 * n_expert_weights)
                act.wait_ge(s_zT, upto(t, c, 1, 1))
                wait_from_one(act, s_lg, upto(t, c))
                fn(xnT[:, :], P[:, P_PREP, :], ACT.Identity, bias=beta_col[:, 0:1], scale=gamma_col[:, 0:1]).then_inc(s_xn, 1)

            def turn_act(t, first, last):
                for n in range(TURN):
                    probs_out(t, n)
                    if not (first and n == 0):
                        context_out(t * TURN + (n - 1))
                    if not (last and n + 1 >= TURN):
                        exps(t + (n + 1) // TURN, (n + 1) % TURN)
                    j, k = n // QUAD, n % QUAD
                    if k == 0 and not (last and j == 1):
                        prep_k(t + (j + 1) // 2, (j + 1) % 2)
                    if k == 1:
                        log_std(t, j - 1)
                        exp_of_gap(t, j - 3)
                    if k == 2:
                        xn_out(t, j - 2)
                    if k == 2 and not last:
                        prep_xT(t + 1, j)
                    if k == 3 and not last:
                        prep_q(t + 1, j)
                    raw_out(t, n)

            prep_xT(0, 0)
            prep_q(0, 0)
            prep_k(0, 0)
            prep_xT(0, 1)
            prep_q(0, 1)
            exps(0, 0)
            turn_act(0, True, False)
            turn_act(1, False, False)
            with act.Fori(2, TURNS - 1) as t:
                turn_act(t, False, False)
            turn_act(TURNS - 1, False, True)
            context_out(G - 1)

            for c in range(3):
                log_std(TURNS, c - 1)
                exp_of_gap(TURNS, c - 3)
                xn_out(TURNS, c - 2)

            def tile_xn(lap, b):
                act.wait_ge(s_tT, lap * RING + (b + 1))
                wait_from_one(act, s_th, (lap * RING + (b - RING + 1)) * CH)
                fn(t_xnT[:, b, :], P[:, P_TT + b % 2, 0:128], ACT.Identity, bias=beta_col[:, 0:1],
                   scale=gamma_col[:, 0:1]).then_inc(s_txn, 1)

            def tile_gelu(lap, b):
                wait_from_one(act, s_ty, lap * RING + (b - RING + 1))
                for c in range(CH):
                    act.wait_ge(s_th, lap * (RING * CH) + (b * CH + c + 1))
                    last = fn(t_hid[:, b, c, :], P[:, P_TH + b % 2 * CH + c, 0:128], ACT.Gelu,
                              bias=tw[:, b, EW_B1 + c:EW_B1 + c + 1])
                last.then_inc(s_tg, 1)

            def slot_act(lap, b):
                for step, lag in ((tile_xn, 0), (tile_gelu, 1)):
                    tile = before_tile(lap, b, lag)
                    if not no_tile(*tile):
                        step(*tile)

            tile_slots(act, slot_act, 1)

            def store(q):
                act.wait_ge(s_w2, 16 * n_expert_weights)
                act.wait_ge(s_add, q * (2 * QUAD) + 2 * QUAD)
                act.dma_start(out_q[q], X[:, bass.ds(q * QUAD, QUAD), :]).then_inc(s_out, 16)

            with act.Fori(0, QUADS) as q:
                store(q)
            act.wait_ge(s_out, 16 * QUADS)

        @block.vector
        def _(dve):
            v = nc.vector
            chain = [0]

            def then(ins):
                chain[0] += 1
                ins.then_inc(s_ln, 1)
                dve.wait_ge(s_ln, chain[0])

            v.memset(ones_row[:, :], 1.0).then_inc(s_ones, 1)
            for j in range(2):
                v.memset(k_diag[:, j].rearrange("p k h m -> p (k h m)"), 0.0).then_inc(s_kd_zero, 1)
            then(v.memset(v_slots[:, :, :, :, :].rearrange("p b k h s -> p (b k h s)"), 0.0))
            v.memset(v_slots[:, :, :, :, HD:HD + 1].rearrange("p b k h s -> p (b k h) s"), 1.0).then_inc(s_v_ones, 1)

            def mean_and_m2():
                me, mo = stats[:, :, 1], stats[:, :, 4]
                then(v.tensor_tensor(tmp_b[:, :], me, mo, ALU.subtract))
                then(v.tensor_scalar(tmp_b[:, :], tmp_b[:, :], 0.5, None, ALU.mult))
                then(v.tensor_tensor(tmp_b[:, :], tmp_b[:, :], tmp_b[:, :], ALU.mult))
                then(v.tensor_tensor(mean[:, :], me, mo, ALU.add))
                then(v.tensor_scalar(mean[:, :], mean[:, :], 0.5, None, ALU.mult))
                then(v.tensor_tensor(tmp_a[:, :], stats[:, :, 2], stats[:, :, 5], ALU.add))
                then(v.scalar_tensor_tensor(out=tmp_a[:, :], in0=tmp_a[:, :], scalar=1.0 / D, in1=tmp_b[:, :],
                                            op0=ALU.mult, op1=ALU.add))

            for t in range(TURNS):
                dve.wait_ge(s_x[t], 16)
                for g in range(t * TURN, (t + 1) * TURN):
                    last = v.bn_stats(stats[:, g, :], X[:, g, :])
            last.then_inc(s_stat, 1)
            dve.wait_ge(s_stat, 1)
            mean_and_m2()
            v.tensor_scalar(tmp_a[:, :], tmp_a[:, :], EPS, None, ALU.add).then_inc(s_var, 1)
            dve.wait_ge(s_w1, 16 * n_attn_weights)
            v.tensor_copy(bv_wide[:, :], bv_col[:, 0:1].to_broadcast([128, 128])).then_inc(s_bvw, 1)
            dve.wait_ge(s_std, 1)
            v.reciprocal(rstd[:, :], tmp_b[:, :]).then_inc(s_rstd, 1)
            dve.wait_ge(s_ab_mm, 1)
            v.tensor_copy(attn_bias[:, :], P[:, P_CTX, 0:D]).then_inc(s_ab, 1)
            v.tensor_copy(br_wide[:, :, :].rearrange("p k e -> p (k e)"), P[:, P_CTX, R_LOGIT:R_RANK]).then_inc(s_br, 1)
            dve.wait_ge(s_const, 11)
            then(v.tensor_copy(base[:, :], region[:, :]))

            def mask(t, j):
                dve.wait_ge(s_adj[j], t * 16 + 16)
                wait_from_one(dve, s_sc, t * 16 + (8 * j - 8))
                v.tensor_scalar(mask_bias[:, j], adj_raw[:, j], 0.0, MASKED, ALU.is_equal, ALU.mult).then_inc(s_mask, 1)

            def v_out(t, j):
                dve.wait_ge(s_vmm, t * 2 + j + 1)
                wait_from_one(dve, s_pv, t * TURN + (QUAD * j - QUAD))
                v.tensor_copy(v_slots[:, j, :, :, 0:HD].rearrange("p k h d -> p (k h) d"),
                              P[:, P_PREP, :].rearrange("p (a d) -> p a d", d=HD)).then_inc(s_v, 1)

            def score_banks(n):
                first = P_SCORES + 2 * (n % 2)
                return P[:, first:first + 2, :].rearrange("p b (h m) -> p (b h) m", h=HALF)

            def maxima(t, n):
                dve.wait_ge(s_sc, (t * TURN + n) * 2 + 2)
                if n == 0:
                    wait_from_one(dve, s_edge, t)
                v.reduce_max(row_max[:, n, :], score_banks(n), AX).then_inc(s_max, 1)

            def less_max(t, n):
                dve.wait_ge(s_max, t * TURN + n + 1)
                wait_from_one(dve, s_pT, (t * TURN + n) * 2 - 2)
                m = row_max[:, n, :].unsqueeze(2).to_broadcast([128, HEADS, N])
                v.tensor_tensor(probs[:, n % 2], score_banks(n), m, ALU.subtract).then_inc(s_sub, 1)

            def normalise(g):
                dve.wait_ge(s_back, g + 1)
                back = P[:, P_CTX, 0:256].rearrange("p (h s) -> p h s", s=SLOT)
                v.reciprocal(rden[:, :], back[:, :, HD]).then_inc(s_rden, 1)
                dve.wait_ge(s_rden, g + 1)
                v.tensor_tensor(ctxn[:, :, :], back[:, :, 0:HD], rden[:, :].unsqueeze(2).to_broadcast([128, HEADS, HD]),
                                ALU.mult).then_inc(s_norm, 1)

            def residual(t, n):
                g = t * TURN + n
                dve.wait_ge(s_wo, g + 1)
                dve.wait_ge(s_xc, t * 2 + n // QUAD + 1)
                xg = X[:, bass.ds(g, 1), :].rearrange("p a d -> p (a d)")
                v.tensor_tensor(xg, P[:, P_CTX, 0:D], xg, ALU.add).then_inc(s_res, 1)
                dve.wait_ge(s_ab, 1)
                dve.wait_ge(s_res, g + 1)
                v.bn_stats(stats2[:, n // QUAD, n % QUAD, :], xg).then_inc(s_st2, 1)

            def flag_rows(t):
                dve.wait_ge(s_max, t * TURN + TURN)
                v.tensor_scalar(no_edge[:, bass.ds(t * TURN, TURN)], row_max[:, :, 0], EMPTY_ROW, HUGE, ALU.is_le,
                                ALU.mult).then_inc(s_edge, 1)

            def variance(t, c):
                if missing(t, c):
                    return
                r = c % 2
                me, mo = stats2[:, r, :, 1], stats2[:, r, :, 4]
                dve.wait_ge(s_st2, upto(t, c, QUAD, QUAD))
                v.tensor_tensor(mean_gap[:, :], me, mo, ALU.subtract).then_inc(s_ln2, 1)
                v.tensor_tensor(m2_sum[:, :], stats2[:, r, :, 2], stats2[:, r, :, 5], ALU.add).then_inc(s_ln2, 1)
                v.tensor_tensor(mean_sum[:, :], me, mo, ALU.add).then_inc(s_ln2, 1)
                dve.wait_ge(s_ln2, upto(t, c, 7, 3))
                v.scalar_tensor_tensor(out=mean_gap[:, :], in0=mean_gap[:, :], scalar=0.25, in1=mean_gap[:, :],
                                       op0=ALU.mult, op1=ALU.mult).then_inc(s_ln2, 1)
                wait_from_one(dve, s_z, upto(t, c, 1, -1))
                v.tensor_scalar(mean2[:, r, :], mean_sum[:, :], 0.5, None, ALU.mult)
                dve.wait_ge(s_ln2, upto(t, c, 7, 4))
                v.scalar_tensor_tensor(out=m2_sum[:, :], in0=m2_sum[:, :], scalar=1.0 / D, in1=mean_gap[:, :],
                                       op0=ALU.mult, op1=ALU.add).then_inc(s_ln2, 1)
                dve.wait_ge(s_ln2, upto(t, c, 7, 5))
                v.tensor_scalar(var2[:, :], m2_sum[:, :], 1.0 + EPS, EPS * EPS, ALU.mult, ALU.add).then_inc(s_var2, 1)

            def refine(t, c):
                if missing(t, c):
                    return
                dve.wait_ge(s_guess, upto(t, c, 1, 1))
                dve.wait_ge(s_var2, upto(t, c, 1, 1))
                v.tensor_tensor(newton[:, :], guess[:, :], guess[:, :], ALU.mult).then_inc(s_ln2, 1)
                dve.wait_ge(s_ln2, upto(t, c, 7, 6))
                v.scalar_tensor_tensor(out=newton[:, :], in0=newton[:, :], scalar=-0.5, in1=var2[:, :],
                                       op0=ALU.mult, op1=ALU.mult).then_inc(s_ln2, 1)
                dve.wait_ge(s_ln2, upto(t, c, 7, 7))
                v.scalar_tensor_tensor(out=rstd2[:, c % 2, :], in0=newton[:, :], scalar=1.5, in1=guess[:, :],
                                       op0=ALU.add, op1=ALU.mult).then_inc(s_rstd2, 1)

            def route(t, c):
                if missing(t, c):
                    return
                r = c % 2
                dve.wait_ge(s_lg, upto(t, c, 1, 1))
                v.tensor_tensor(logit[:, :, :], P[:, P_CTX, R_LOGIT:R_RANK].rearrange("p (k e) -> p k e", e=E),
                                br_wide[:, :, :], ALU.add).then_inc(s_logit, 1)
                dve.wait_ge(s_br, 1)
                dve.wait_ge(s_logit, upto(t, c, 1, 1))
                for k in range(QUAD):
                    last = v.max(top[:, k, :], logit[:, k, :])
                last.then_inc(s_rt, 1)
                dve.wait_ge(s_rt, upto(t, c, 4, 1))
                wait_from_one(dve, s_eg, upto(t, c))
                v.tensor_tensor(gap[:, :], top[:, :, 1], top[:, :, 0], ALU.subtract).then_inc(s_gap, 1)
                for k in range(QUAD):
                    last = v.max_index(top_i[:, k, :], top[:, k, :], logit[:, k, :])
                last.then_inc(s_rt, 1)
                dve.wait_ge(s_rt, upto(t, c, 4, 2))
                v.tensor_copy(top_f[:, :, :], top_i[:, :, 0:2]).then_inc(s_rt, 1)
                dve.wait_ge(s_rt, upto(t, c, 4, 3))
                for i in range(2):
                    last = v.tensor_tensor(pick[:, i], iota_e[:, :].unsqueeze(1).to_broadcast([128, QUAD, E]),
                                           top_f[:, :, i].unsqueeze(2).to_broadcast([128, QUAD, E]), ALU.is_equal)
                last.then_inc(s_rt, 1)
                v.tensor_copy(token_row[:, r, :, D + 1], top_f[:, :, 0])
                dve.wait_ge(s_rt, upto(t, c, 4, 4))
                wait_from_one(dve, s_rank, upto(t, c))
                v.tensor_tensor(picked[:, :, :], pick[:, 0], pick[:, 1], ALU.add).then_inc(s_pick, 1)

            def places(t, c):
                if missing(t, c):
                    return
                dve.wait_ge(s_rank, upto(t, c, 1, 1))
                v.tensor_tensor(place[:, :, :], P[:, P_CTX, R_RANK:R_TOTAL].rearrange("p (k e) -> p k e", e=E),
                                base[:, :].unsqueeze(1).to_broadcast([128, QUAD, E]), ALU.add).then_inc(s_pl, 1)
                dve.wait_ge(s_pl, upto(t, c, 4, 1))
                v.tensor_tensor(base[:, :], P[:, P_CTX, R_TOTAL:R_TOTAL + E], base[:, :], ALU.add).then_inc(s_pl, 1)
                dve.wait_ge(s_pl, upto(t, c, 4, 2))
                v.tensor_tensor(placed[:, :, :, :], pick[:, :, :, :], place[:, :, :].unsqueeze(1).to_broadcast([128, 2, QUAD, E]),
                                ALU.mult).then_inc(s_pl, 1)
                dve.wait_ge(s_pl, upto(t, c, 4, 3))
                v.reduce_sum(place_f[:, :, :], placed[:, :, :, :], AX).then_inc(s_pl, 1)
                dve.wait_ge(s_pl, upto(t, c, 4, 4))
                v.tensor_copy(place_i[:, c % 2], place_f[:, :, :]).then_inc(s_place, 1)

            def turn_dve(t, first, last):
                for n in range(TURN):
                    if n == TURN - 1:
                        flag_rows(t)
                    prev = not (first and n == 0)
                    more = not (last and n + 1 >= TURN)
                    nxt = (t + (n + 1) // TURN, (n + 1) % TURN)
                    j, k = n // QUAD, n % QUAD
                    if more:
                        maxima(*nxt)
                    if prev:
                        normalise(t * TURN + (n - 1))
                    if more:
                        less_max(*nxt)
                    if k == 0 and not (last and j == 1):
                        mask(t + (j + 1) // 2, (j + 1) % 2)
                    if prev:
                        residual(*((t, n - 1) if n else (t - 1, TURN - 1)))
                    if k == 1 and not (last and j == 1):
                        v_out(t + (j + 1) // 2, (j + 1) % 2)
                    if k == 0:
                        variance(t, j - 1)
                        route(t, j - 3)
                    if k == 1:
                        refine(t, j - 1)
                    if k == 2:
                        places(t, j - 3)

            mask(0, 0)
            dve.wait_ge(s_v_ones, 1)
            v_out(0, 0)
            maxima(0, 0)
            less_max(0, 0)
            turn_dve(0, True, False)
            turn_dve(1, False, False)
            with dve.Fori(2, TURNS - 1) as t:
                turn_dve(t, False, False)
            turn_dve(TURNS - 1, False, True)
            normalise(G - 1)
            residual(TURNS - 1, TURN - 1)

            for c in range(3):
                variance(TURNS, c - 1)
                route(TURNS, c - 3)
                refine(TURNS, c - 1)
                places(TURNS, c - 3)

            tables = [0]

            def next_table(ins):
                tables[0] += 1
                ins.then_inc(s_tb, 1)
                dve.wait_ge(s_tb, tables[0])

            dve.wait_ge(s_pl, 4 * QUADS)
            v.tensor_tensor(pad_i[:, :], base[:, :], part_f[:, 0:1].to_broadcast([128, E]), ALU.add).then_inc(s_pad, 1)
            next_table(v.scalar_tensor_tensor(out=count_i[:, :], in0=base[:, :], scalar=127.0, in1=region[:, :],
                                              op0=ALU.add, op1=ALU.subtract))
            next_table(v.tensor_scalar(tiles_i[:, :], count_i[:, :], 7, None, ALU.logical_shift_right))
            next_table(v.tensor_copy(tiles_of[:, :], tiles_i[:, :]))
            v.tensor_scalar(skip[:, :], tiles_of[:, :], -128.0, float(REGION), ALU.mult, ALU.add)
            next_table(v.tensor_copy(tiles_upto[:, 0:1], tiles_of[:, 0:1]))
            for e in range(1, E):
                next_table(v.tensor_tensor(tiles_upto[:, e:e + 1], tiles_upto[:, e - 1:e], tiles_of[:, e:e + 1], ALU.add))
            v.tensor_scalar(tile_row[:, :], tile_no[:, :], 128.0, None, ALU.mult)
            next_table(v.tensor_scalar(tile_e[:, :], tile_no[:, :], tiles_upto[:, 0:1], None, ALU.is_ge))
            for e in range(E):
                if e:
                    v.scalar_tensor_tensor(out=tile_e[:, :], in0=tile_no[:, :], scalar=tiles_upto[:, e:e + 1],
                                           in1=tile_e[:, :], op0=ALU.is_ge, op1=ALU.add)
                next_table(v.tensor_scalar(tile_tmp[:, e % 2, :], tile_no[:, :], tiles_upto[:, e:e + 1], skip[:, e:e + 1],
                                           ALU.is_ge, ALU.mult))
                next_table(v.tensor_tensor(tile_row[:, :], tile_row[:, :], tile_tmp[:, e % 2, :], ALU.add))
            v.tensor_copy(tile_row_i[:, :], tile_row[:, :])
            v.tensor_scalar(tile_e_i[:, :], tile_e[:, :], float(E - 1), None, ALU.min).then_inc(s_tab, 1)
            dve.wait_ge(s_tab, 1)

            def tile_out(lap, b):
                dve.wait_ge(s_ty, lap * RING + (b + 1))
                dve.wait_ge(s_tw, lap * RING + (b + 1))
                dve.wait_ge(s_to, lap * RING + (b + 1))
                wait_from_one(dve, s_ys[b], lap * 16)
                v.tensor_copy(to_i[:, b:b + 1], to_f[:, b:b + 1])
                v.tensor_tensor(t_y[:, b, :], P[:, P_TY + b % 2, 0:D], tw[:, b, EW_B2:EW_B2 + D], ALU.add).then_inc(s_y[b], 1)

            def tile_weights(lap, b):
                e = dve.value_load(tile_e_i[0:1, bass.ds(lap * RING + b, 1)], min_val=0, max_val=E - 1)
                wait_from_one(dve, s_y[b], lap)
                wait_from_one(dve, s_ty, lap * RING + (b - RING + 1))
                v.tensor_copy(tw[:, b, :], ew[:, bass.ds(e, 1), :].rearrange("p a c -> p (a c)")).then_inc(s_tw, 1)

            def tile_to(lap, b):
                dve.wait_ge(s_load[b], lap * 16 + 16)
                wait_from_one(dve, s_y[b], lap)
                v.scalar_tensor_tensor(out=to_f[:, b:b + 1], in0=t_row[:, b, D + 1:D + 2], scalar=tile_e[:, bass.ds(lap * RING + b, 1)],
                                       in1=t_row[:, b, D:D + 1], op0=ALU.not_equal, op1=ALU.add).then_inc(s_to, 1)

            def slot_dve(lap, b):
                for step, lag in ((tile_out, 4), (tile_to, 0), (tile_weights, 0)):
                    tile = before_tile(lap, b, lag)
                    if not no_tile(*tile):
                        step(*tile)

            tile_slots(dve, slot_dve, 4)

            gate_steps = [0]

            def next_gate(ins):
                gate_steps[0] += 1
                ins.then_inc(s_gt, 1)
                dve.wait_ge(s_gt, gate_steps[0])

            dve.wait_ge(s_eg, QUADS)
            dve.wait_ge(s_edge, TURNS)
            v.tensor_scalar(tmp_a[:, :], exp_gap[:, :], 1.0, None, ALU.add)
            next_gate(v.tensor_scalar(no_edge[:, :], no_edge[:, :], HUGE, 0.0, ALU.mult, ALU.mult))
            next_gate(v.reciprocal(tmp_b[:, :], tmp_a[:, :]))
            next_gate(v.tensor_tensor(gates[:, 0], tmp_b[:, :], no_edge[:, :], ALU.add))
            next_gate(v.tensor_tensor(gates[:, 1], gates[:, 0], exp_gap[:, :], ALU.mult))

            def add_both(lap, b):
                dve.wait_ge(s_both[b], lap * 16 + 16)
                for i in range(2):
                    for k in range(QUAD):
                        g = lap * (RING * QUAD) + (b * QUAD + k)
                        xg = X[:, bass.ds(g, 1), :].rearrange("p a d -> p (a d)")
                        if i:
                            dve.wait_ge(s_add, lap * (RING * 2 * QUAD) + (b * 2 * QUAD + k + 1))
                        v.scalar_tensor_tensor(out=xg, in0=both[:, b, k, i * D:(i + 1) * D], scalar=gates[:, i, bass.ds(g, 1)],
                                               in1=xg, op0=ALU.mult, op1=ALU.add).then_inc(s_add, 1)

            with dve.Fori(0, QUADS // RING) as lap:
                for b in range(RING):
                    add_both(lap, b)



_INS = ["x", "adj", "L0_gnn_Wq", "L0_gnn_bq", "L0_gnn_Wk", "L0_gnn_bk", "L0_gnn_Wv", "L0_gnn_bv", "L0_gnn_Wo",
        "L0_gnn_bo", "L0_ffn_gamma", "L0_ffn_beta", "L0_ffn_Wr", "L0_ffn_br", "L0_ffn_W1", "L0_ffn_b1", "L0_ffn_W2",
        "L0_ffn_b2"]


def kernel(**inputs):
    import numpy as _np
    import concourse.bacc as _bacc
    from concourse import mybir as _mybir
    from concourse.bass_utils import run_bass_kernel_spmd as _run

    nc = _bacc.Bacc("TRN2", target_bir_lowering=False, num_devices=1)
    arrays, args = {}, []
    for name in _INS:
        a = _np.ascontiguousarray(inputs[name])
        arrays[f"in_{name}_dram"] = a
        args.append(nc.dram_tensor(f"in_{name}_dram", a.shape, _mybir.dt.from_np(a.dtype), kind="ExternalInput").ap())
    out = nc.dram_tensor("out_0_dram", inputs["x"].shape, _mybir.dt.float32, kind="ExternalOutput").ap()
    build(nc, *args, out)
    r = _run(nc, [arrays], core_ids=[0])
    return r.results[0]["out_0_dram"]
```

```python
from contextlib import ExitStack

import concourse.bass as bass
from concourse import mybir

F32 = mybir.dt.float32
BF16 = mybir.dt.bfloat16
I32 = mybir.dt.int32
U32 = mybir.dt.uint32
ALU = mybir.AluOpType
ACT = mybir.ActivationFunctionType
AX = mybir.AxisListType.X

MASKED = -1.0e30
EMPTY_ROW = -5.0e29
HUGE = 3.0e38
EPS = 1e-05
HEADS = 8
QUAD = 4
TURN = 8
SLOT = 32
BLOCKS = 2
TILE = 128 * BLOCKS
RING = 4
SUM_RING = 8


def wait_from_one(engine, semaphore, value):
    if isinstance(value, int) and value <= 0:
        return
    engine.wait_ge(semaphore, value)


def build(nc, x, adj, Wq, bq, Wk, bk, Wv, bv, Wo, bo, gamma, beta, Wr, br, W1, b1, W2, b2, out):
    G, N, D = x.shape
    E, _, HID = W1.shape
    HD = D // HEADS
    CH = HID // 128
    HALF = HEADS // 2
    TURNS = G // TURN
    QUADS = G // QUAD
    TOKENS = G * N
    ROW = D + 2
    REGION = TOKENS + TILE
    TILES = (2 * TOKENS + E * (TILE - 1)) // TILE
    SPARE = BLOCKS * (TILES - 2 * TOKENS // TILE)
    PADS = BLOCKS * E + SPARE
    TOKEN_STEP = 2 * 2 * QUAD * N
    EW = CH * 128 + CH * D + CH + D
    EW_W2, EW_B1, EW_B2 = CH * 128, CH * 128 + CH * D, CH * 128 + CH * D + CH
    table = nc.dram_tensor("table", [E * REGION + SPARE * 128, ROW], F32, kind="Internal").ap()
    results = nc.dram_tensor("results", [2 * TOKENS + PADS * 128, D], F32, kind="Internal").ap()
    assert N == 128 and D == 128 and W2.shape[2] == D and G % TURN == 0 and E == 8

    with ExitStack() as ctx:
        def sb(name, shape, dt=F32):
            return ctx.enter_context(nc.sbuf_tensor(name, shape, dt))

        def sem(name):
            return ctx.enter_context(nc.semaphore(name))

        X = sb("X", [128, G, D])
        ident = sb("ident", [128, 128])
        identb = sb("identb", [128, 128], BF16)
        ones_row = sb("ones_row", [1, 128])
        wq = sb("wq", [D, D])
        wk = sb("wk", [D, D])
        wv = sb("wv", [D, D])
        wo = sb("wo", [D, D])
        bq_col = sb("bq_col", [D, 1])
        bk_col = sb("bk_col", [D, 1])
        bv_col = sb("bv_col", [D, 1])
        bv_wide = sb("bv_wide", [D, 128])
        bo_row = sb("bo_row", [1, D])
        attn_bias = sb("attn_bias", [128, D])
        gamma_col = sb("gamma_col", [D, 1])
        beta_col = sb("beta_col", [D, 1])
        wr = sb("wr", [D, E])
        br_row = sb("br_row", [1, E])
        iota_e = sb("iota_e", [128, E])
        stats = sb("stats", [128, G, 6])
        mean = sb("mean", [128, G])
        rstd = sb("rstd", [128, G])
        tmp_a = sb("tmp_a", [128, G])
        tmp_b = sb("tmp_b", [128, G])
        tmp_c = sb("tmp_c", [128, G])
        stats2 = sb("stats2", [128, 2, QUAD, 6])
        mean2 = sb("mean2", [128, 2, QUAD])
        mean_sum = sb("mean_sum", [128, QUAD])
        mean_gap = sb("mean_gap", [128, QUAD])
        m2_sum = sb("m2_sum", [128, QUAD])
        var2 = sb("var2", [128, QUAD])
        ln_var = sb("ln_var", [128, QUAD])
        guess = sb("guess", [128, QUAD])
        newton = sb("newton", [128, QUAD])
        rstd2 = sb("rstd2", [128, 2, QUAD])
        adj_raw = sb("adj_raw", [128, 2, QUAD, N], I32)
        mask_bias = sb("mask_bias", [128, 2, QUAD, N], BF16)
        xhat = sb("xhat", [128, QUAD, D])
        xT = sb("xT", [D, QUAD * N])
        qT = sb("qT", [D, 2, QUAD * N])
        kT = sb("kT", [D, QUAD * N])
        k_diag = sb("k_diag", [D, 2, QUAD, HEADS, N])
        v_slots = sb("v_slots", [128, 2, QUAD, HEADS, SLOT])
        probs = sb("probs", [128, 2, HEADS, N])
        probsT = sb("probsT", [128, HEADS, N])
        row_max = sb("row_max", [128, TURN, HEADS])
        no_edge = sb("no_edge", [128, G])
        ctxT_raw = sb("ctxT_raw", [128, 2 * N])
        rden = sb("rden", [128, HEADS])
        ctxn = sb("ctxn", [128, HEADS, HD])
        ctxT = sb("ctxT", [D, N])
        token_row = sb("token_row", [128, 2, QUAD, ROW])
        last_row = sb("last_row", [128, QUAD, ROW])
        token_step = sb("token_step", [128, QUAD])
        z_mid = sb("z_mid", [128, QUAD, D])
        xnT = sb("xnT", [D, QUAD * N])
        br_wide = sb("br_wide", [128, QUAD, E])
        logit = sb("logit", [128, QUAD, E])
        top = sb("top", [128, QUAD, E])
        top_i = sb("top_i", [128, QUAD, E], U32)
        top_f = sb("top_f", [128, QUAD, 2])
        gap = sb("gap", [128, QUAD])
        exp_gap = sb("exp_gap", [128, G])
        gates = sb("gates", [128, 2, G])
        pick = sb("pick", [128, 2, QUAD, E])
        picked = sb("picked", [128, QUAD, E], BF16)
        before = sb("before", [128, 128], BF16)
        all_ones = sb("all_ones", [128, 128], BF16)
        base = sb("base", [128, E])
        rank = sb("rank", [128, (QUAD + 1) * E])
        place = sb("place", [128, QUAD, E])
        placed = sb("placed", [128, 2, QUAD, E])
        place_f = sb("place_f", [128, 2, QUAD])
        place_i = sb("place_i", [128, 2, 2, QUAD], U32)
        pad_row = sb("pad_row", [128, PADS, ROW])
        pad_i = sb("pad_i", [128, E], I32)
        region = sb("region", [128, E])
        count_i = sb("count_i", [128, E], I32)
        tiles_i = sb("tiles_i", [128, E], I32)
        tiles_of = sb("tiles_of", [128, E])
        tiles_upto = sb("tiles_upto", [128, E])
        skip = sb("skip", [128, E])
        tile_no = sb("tile_no", [128, TILES])
        tile_e = sb("tile_e", [128, TILES])
        tile_row = sb("tile_row", [128, TILES])
        behind = sb("behind", [128, 2, TILES, E])
        tile_skip = sb("tile_skip", [128, TILES])
        tile_e_i = sb("tile_e_i", [128, TILES], I32)
        tile_row_i = sb("tile_row_i", [128, TILES], I32)
        ew = sb("ew", [128, E, EW])
        tw = sb("tw", [128, RING, EW])
        t_row = sb("t_row", [128, RING, BLOCKS, ROW])
        t_xnT = sb("t_xnT", [D, RING, TILE])
        t_hid = sb("t_hid", [128, RING, CH, TILE])
        t_y = sb("t_y", [128, RING, BLOCKS, D])
        to_f = sb("to_f", [128, RING, BLOCKS])
        to_i = sb("to_i", [128, RING, BLOCKS], U32)
        both = k_diag[:, :, :, :, :].rearrange("p j k h m -> p (j k h m)").rearrange(
            "p (b k d) -> p b k d", k=QUAD, d=2 * D)
        assert both.shape[1] == SUM_RING

        P = ctx.enter_context(nc.psum_tensor("P", [128, 8, 512], F32))
        P_SCORES, P_T, P_PREP, P_CTX = 0, 4, 6, 7
        R_LOGIT, R_RANK, R_TOTAL = 256, 256 + QUAD * E, 256 + 2 * QUAD * E
        P_TT, P_TH, P_TY = 0, 2, 2 + 2 * CH

        block = ctx.enter_context(nc.Block())

        s_w1 = sem("s_attention_weights_loaded")
        s_w2 = sem("s_expert_weights_loaded")
        s_x = [sem(f"s_x_loaded_{t}") for t in range(TURNS)]
        s_ones = sem("s_ones")
        s_ident0 = sem("s_ident_zeroed")
        s_const = sem("s_constants")
        s_v_ones = sem("s_v_slots_preset")
        s_kd_zero = sem("s_k_diag_zeroed")
        s_stat = sem("s_stats1")
        s_ln = sem("s_ln_chain")
        s_var = sem("s_var_ready")
        s_lnv1 = sem("s_first_ln_var")
        s_std = sem("s_std_guess")
        s_rstd = sem("s_rstd_ready")
        s_ab_mm = sem("s_attn_bias_product")
        s_ab = sem("s_attn_bias")
        s_bvw = sem("s_bv_wide")
        s_adj = [sem(f"s_adj_loaded_{b}") for b in range(2)]
        s_mask = sem("s_mask_bias")
        s_centred = sem("s_x_less_mean")
        s_xhat = sem("s_xhat")
        s_xhatT = sem("s_xhatT")
        s_xT = sem("s_xT")
        s_qmm = sem("s_q_product")
        s_q = sem("s_qT")
        s_kmm = sem("s_k_product")
        s_k = sem("s_kT")
        s_kd = [sem(f"s_k_diag_{b}") for b in range(2)]
        s_vmm = sem("s_v_product")
        s_v = sem("s_v_slots")
        s_sc = sem("s_scores")
        s_max = sem("s_row_max")
        s_edge = sem("s_no_edge")
        s_sub = sem("s_scores_less_max")
        s_exp = sem("s_probs")
        s_pT = sem("s_probsT_psum")
        s_pTe = sem("s_probsT")
        s_pv = sem("s_context_product")
        s_cr = sem("s_ctxT_raw")
        s_back = sem("s_context_back")
        s_rden = sem("s_rden")
        s_norm = sem("s_ctxn")
        s_cT = sem("s_ctxT_psum")
        s_cTe = sem("s_ctxT")
        s_wo = sem("s_out_product")
        s_xc = sem("s_x_plus_bias")
        s_res = sem("s_residual")
        s_st2 = sem("s_stats2")
        s_br = sem("s_br_wide")
        s_ln2 = sem("s_second_norm_chain")
        s_var2 = sem("s_var2")
        s_lnv = sem("s_ln_var")
        s_guess = sem("s_rstd2_guess")
        s_rstd2 = sem("s_rstd2")
        s_zm = sem("s_z_mid")
        s_z = sem("s_z")
        s_z_last = sem("s_z_of_the_last_quad")
        s_zT = sem("s_zT")
        s_xn = sem("s_xnT")
        s_lg = sem("s_logits_product")
        s_logit = sem("s_logits")
        s_rt = sem("s_route_chain")
        s_gap = sem("s_gap")
        s_eg = sem("s_exp_gap")
        s_pick = sem("s_picked")
        s_rank = sem("s_ranks")
        s_rank_out = sem("s_ranks_out")
        s_pl = sem("s_place_chain")
        s_place = sem("s_places")
        s_token = sem("s_token_column")
        s_scat = [sem(f"s_rows_scattered_{b}") for b in range(2)]
        s_pad_set = sem("s_pad_rows_preset")
        s_spare = sem("s_spare_rows_stored")
        s_pad = sem("s_pad_places")
        s_pad_scat = sem("s_pads_scattered")
        s_tb = sem("s_tile_table_chain")
        s_tab = sem("s_tile_tables")
        s_load = [sem(f"s_tile_loaded_{b}") for b in range(RING)]
        s_tw = sem("s_tile_weights")
        s_to = sem("s_tile_destinations")
        s_tT = sem("s_tile_transposed")
        s_txn = sem("s_tile_xnT")
        s_th = sem("s_tile_hidden_product")
        s_tg = sem("s_tile_gelu")
        s_ty = sem("s_tile_product")
        s_y = [sem(f"s_tile_result_{b}") for b in range(RING)]
        s_ys = [sem(f"s_tile_scattered_{b}") for b in range(RING)]
        s_both = [sem(f"s_results_loaded_{b}") for b in range(SUM_RING)]
        s_gt = sem("s_gate_chain")
        s_gates = sem("s_gates")
        s_first = sem("s_first_gated")
        s_second = sem("s_second_gated")
        s_add = sem("s_sum")
        s_out = sem("s_out_stored")

        n_attn_weights, n_expert_weights = 9, 9

        def col(ap):
            return ap.rearrange("(p a) -> p a", a=1)

        def row(ap):
            return ap.rearrange("(a n) -> a n", a=1)

        adj_q = adj.rearrange("(q k) n m -> q n k m", k=QUAD)
        out_q = out.rearrange("(q k) n d -> q n k d", k=QUAD)

        first_norm = (slice(0, TURN), slice(TURN, 2 * TURN), slice(2 * TURN, G))

        def missing(t, c):
            return isinstance(t, int) and not 0 <= 2 * t + c < QUADS

        def upto(t, c, each=1, more=0):
            return t * (2 * each) + (c * each + more)

        def rows_of(t, c):
            if isinstance(t, int) and 2 * t + c == QUADS - 1:
                return last_row
            return token_row[:, c % 2]

        def laps(t, c, each=1, more=0):
            return t * each + (c // 2 * each + more)

        def quad_of(t, c):
            return bass.ds(t * TURN + c * QUAD, QUAD)

        FULL_LAPS = TILES // RING

        def before_tile(lap, b, n):
            return lap + (b - n) // RING, (b - n) % RING

        def no_tile(lap, b):
            return isinstance(lap, int) and not 0 <= RING * lap + b < TILES

        def tile_slots(engine, slot, extra):
            for b in range(RING):
                slot(0, b)
            with engine.Fori(1, FULL_LAPS) as lap:
                for b in range(RING):
                    slot(lap, b)
            for i in range(FULL_LAPS * RING, TILES + extra):
                slot(i // RING, i % RING)

        @block.sync
        def _(sp):
            x_t = x.rearrange("(t g) n d -> t n g d", g=TURN)

            def load_turn(t):
                sp.dma_start(X[:, t * TURN:(t + 1) * TURN, :], x_t[t]).then_inc(s_x[t], 16)

            load_turn(0)
            for dst, src in ((wq[:, :], Wq), (wk[:, :], Wk), (wv[:, :], Wv), (wo[:, :], Wo),
                             (bq_col[:, :], col(bq)), (bk_col[:, :], col(bk)), (bv_col[:, :], col(bv)),
                             (bo_row[:, :], row(bo)), (br_row[:, :], row(br))):
                sp.dma_start(dst, src).then_inc(s_w1, 16)
            for j in range(2):
                sp.dma_start(adj_raw[:, j], adj_q[j]).then_inc(s_adj[j], 16)
            load_turn(1)

            def spread_k(turn, j):
                sp.wait_ge(s_kd_zero, 2)
                sp.wait_ge(s_k, turn * 2 + j + 1)
                for h in range(HEADS):
                    rows = slice(h * HD, (h + 1) * HD)
                    sp.dma_start(k_diag[rows, j, :, h, :], kT[rows, :].rearrange("p (k n) -> p k n", k=QUAD)).then_inc(s_kd[j], 16)

            sp.wait_ge(s_kd_zero, 2)
            spread_k(0, 0)
            for t in range(2, TURNS):
                load_turn(t)
            for dst, src in ((gamma_col[:, :], col(gamma)), (beta_col[:, :], col(beta)), (wr[:, :], Wr),
                             (ew[:, :, 0:HID], W1.rearrange("e d h -> d e h")),
                             (ew[:, :, EW_B2:EW_B2 + D], b2.unsqueeze(0).to_broadcast([128, E, D]))):
                sp.dma_start(dst, src).then_inc(s_w2, 16)
            for c in range(CH):
                sp.dma_start(ew[:, :, EW_W2 + c * D:EW_W2 + (c + 1) * D],
                             W2[:, c * 128:(c + 1) * 128, :].rearrange("e p d -> p e d")).then_inc(s_w2, 16)
                sp.dma_start(ew[:, :, EW_B1 + c:EW_B1 + c + 1], b1[:, c * 128:(c + 1) * 128].rearrange("e (p a) -> p e a", a=1),
                             allow_slow_non_contiguous=True).then_inc(s_w2, 16)
            sp.wait_ge(s_pad_set, 3)
            sp.dma_start(table[E * REGION:E * REGION + SPARE * 128, :].rearrange("(i p) c -> p i c", p=128),
                         pad_row[:, BLOCKS * E:PADS, :]).then_inc(s_spare, 16)

            def turn_sp(t, last):
                for j in range(2):
                    if not (last and j == 1):
                        spread_k(t + (j + 1) // 2, (j + 1) % 2)
                    if not last:
                        sp.wait_ge(s_kd_zero, 2)
                        sp.wait_ge(s_mask, t * 2 + j + 1)
                        sp.dma_start(adj_raw[:, j], adj_q[t * 2 + (j + 2)]).then_inc(s_adj[j], 16)

            turn_sp(0, False)
            with sp.Fori(1, TURNS - 1) as t:
                turn_sp(t, False)
            turn_sp(TURNS - 1, True)

            sp.wait_ge(s_pad, 1)
            for e in range(E):
                first = sp.value_load(pad_i[0:1, e:e + 1], min_val=e * REGION, max_val=e * REGION + TOKENS)
                sp.dma_start(table[bass.ds(first, TILE), :].rearrange("(a p) c -> p a c", p=128),
                             pad_row[:, BLOCKS * e:BLOCKS * (e + 1), :]).then_inc(s_pad_scat, 16)

            def first_row(lap, b):
                return sp.value_load(tile_row_i[0:1, bass.ds(lap * RING + b, 1)], min_val=0,
                                     max_val=E * REGION + SPARE * 128 - TILE)

            def load_rows(b, first):
                rows = table[bass.ds(first, TILE), :].rearrange("(a p) c -> p a c", p=128)
                sp.dma_start(t_row[:, b], rows).then_inc(s_load[b], 16)

            def load_tile(lap, b):
                first = first_row(lap, b)
                wait_from_one(sp, s_tT, lap * RING + (b - RING + 1))
                wait_from_one(sp, s_to, lap * RING + (b - RING + 1))
                load_rows(b, first)

            sp.wait_ge(s_tab, 1)
            firsts = [first_row(0, b) for b in range(RING)]
            for r in range(2):
                sp.wait_ge(s_scat[r], 16 * 2 * QUAD * (QUADS // 2))
            sp.wait_ge(s_spare, 16)
            sp.wait_ge(s_pad_scat, 16 * E)
            for b in range(RING):
                load_rows(b, firsts[b])
            with sp.Fori(1, FULL_LAPS) as lap:
                for b in range(RING):
                    load_tile(lap, b)
            for i in range(FULL_LAPS * RING, TILES):
                load_tile(i // RING, i % RING)

            for b in range(RING):
                sp.wait_ge(s_ys[b], 16 * BLOCKS * len(range(b, TILES, RING)))
            pairs = results[0:2 * TOKENS, :].rearrange("(q k n i) d -> q n k (i d)", k=QUAD, n=N, i=2)

            def load_both(lap, b):
                sp.dma_start(both[:, b], pairs[lap * SUM_RING + b]).then_inc(s_both[b], 16)

            def store(lap, b):
                sp.wait_ge(s_spare, 16)
                sp.wait_ge(s_add, lap * SUM_RING + (b + 1))
                q = lap * SUM_RING + b
                sp.dma_start(out_q[q], X[:, bass.ds(q * QUAD, QUAD), :]).then_inc(s_out, 16)

            for b in range(SUM_RING):
                load_both(0, b)
            with sp.Fori(0, QUADS // SUM_RING - 1) as lap:
                for b in range(SUM_RING):
                    store(lap, b)
                    load_both(lap + 1, b)
            for b in range(SUM_RING):
                store(QUADS // SUM_RING - 1, b)
            sp.wait_ge(s_out, 16 * QUADS)

        @block.gpsimd
        def _(pool):
            nc.gpsimd.memset(ident[:, :], 0.0).then_inc(s_ident0, 1)
            nc.gpsimd.memset(identb[:, :], 0.0).then_inc(s_ident0, 1)
            pool.wait_ge(s_ident0, 2)
            for m in (ident, identb):
                nc.gpsimd.affine_select(out=m[:, :], in_=m[:, :], compare_op=ALU.not_equal, fill=1.0, base=0,
                                        pattern=[[-1, 128]], channel_multiplier=1).then_inc(s_const, 1)
            nc.gpsimd.memset(k_diag[:, 0].rearrange("p k h m -> p (k h m)"), 0.0).then_inc(s_kd_zero, 1)

            def normalise(t, j):
                quad = bass.ds(t * TURN + QUAD * j, QUAD)
                wide = [128, QUAD, D]
                batches = min(t + 1, 3) if isinstance(t, int) else 3
                pool.wait_ge(s_rstd, batches)
                wait_from_one(pool, s_xhatT, t * 2 + j)
                nc.gpsimd.tensor_tensor(xhat[:, :, :], X[:, quad, :], mean[:, quad].unsqueeze(2).to_broadcast(wide),
                                        ALU.subtract).then_inc(s_centred, 1)
                pool.wait_ge(s_rstd, batches)
                pool.wait_ge(s_centred, t * 2 + j + 1)
                nc.gpsimd.tensor_tensor(xhat[:, :, :], xhat[:, :, :], rstd[:, quad].unsqueeze(2).to_broadcast(wide),
                                        ALU.mult).then_inc(s_xhat, 1)
                pool.wait_ge(s_ab, 1)
                nc.gpsimd.tensor_tensor(X[:, quad, :], X[:, quad, :], attn_bias[:, :].unsqueeze(1).to_broadcast(wide),
                                        ALU.add).then_inc(s_xc, 1)

            def normalise2(t, c):
                if missing(t, c):
                    return
                r, wide = c % 2, [128, QUAD, D]
                pool.wait_ge(s_const, 11)
                pool.wait_ge(s_rstd2, upto(t, c, 1, 1))
                nc.gpsimd.tensor_tensor(z_mid[:, :, :], X[:, quad_of(t, c), :], mean2[:, r, :].unsqueeze(2).to_broadcast(wide),
                                        ALU.subtract).then_inc(s_zm, 1)
                pool.wait_ge(s_zm, upto(t, c, 1, 1))
                wait_from_one(pool, s_scat[r], laps(t, c, 16 * 2 * QUAD))
                nc.gpsimd.tensor_tensor(token_row[:, r, :, 0:D], z_mid[:, :, :], rstd2[:, r, :].unsqueeze(2).to_broadcast(wide),
                                        ALU.mult).then_inc(s_z, 1)

            def scatter(t, c):
                if missing(t, c):
                    return
                r = c % 2
                pool.wait_ge(s_place, upto(t, c, 1, 1))
                rows = rows_of(t, c)
                nc.gpsimd.tensor_tensor(rows[:, :, D], rows[:, :, D], token_step[:, :], ALU.add).then_inc(s_token, 1)
                pool.wait_ge(s_const, 11)
                pool.wait_ge(s_token, upto(t, c, 1, 1))
                for i in range(2):
                    for k in range(QUAD):
                        nc.gpsimd.indirect_dma_start(
                            out=table, out_offset=bass.IndirectOffsetOnAxis(ap=place_i[:, r, i, k:k + 1], axis=0),
                            in_=rows[:, k, :], in_offset=None).then_inc(s_scat[r], 16)

            normalise(0, 0)
            normalise(0, 1)
            nc.gpsimd.iota(iota_e[:, :], pattern=[[1, E]], base=0, channel_multiplier=0,
                           allow_small_or_imprecise_dtypes=True).then_inc(s_const, 1)
            all_rows = pad_row[:, :, :].rearrange("p i c -> p (i c)")
            nc.gpsimd.memset(all_rows, 0.0).then_inc(s_pad_set, 1)
            nc.gpsimd.memset(all_ones[:, :], 1.0).then_inc(s_const, 1)
            nc.gpsimd.memset(token_step[:, :], float(TOKEN_STEP)).then_inc(s_const, 1)
            nc.gpsimd.iota(region[:, :], pattern=[[REGION, E]], base=0, channel_multiplier=0,
                           allow_small_or_imprecise_dtypes=True).then_inc(s_const, 1)
            nc.gpsimd.iota(tile_no[:, :], pattern=[[1, TILES]], base=0, channel_multiplier=0,
                           allow_small_or_imprecise_dtypes=True).then_inc(s_const, 1)
            for r in range(2):
                nc.gpsimd.iota(token_row[:, r, :, D], pattern=[[2 * N, QUAD]], base=r * QUAD * N * 2 - TOKEN_STEP,
                               channel_multiplier=2, allow_small_or_imprecise_dtypes=True).then_inc(s_const, 1)
            nc.gpsimd.iota(last_row[:, :, D], pattern=[[2 * N, QUAD]], base=(QUADS - 1) * QUAD * N * 2 - TOKEN_STEP,
                           channel_multiplier=2, allow_small_or_imprecise_dtypes=True).then_inc(s_const, 1)
            pool.wait_ge(s_const, 10)
            nc.gpsimd.affine_select(out=before[:, :], in_=all_ones[:, :], compare_op=ALU.is_gt, fill=0.0, base=0,
                                    pattern=[[1, 128]], channel_multiplier=-1).then_inc(s_const, 1)
            pool.wait_ge(s_pad_set, 1)
            nc.gpsimd.iota(pad_row[:, :, D], pattern=[[128, PADS]], base=2 * TOKENS - 1, channel_multiplier=1,
                           allow_small_or_imprecise_dtypes=True).then_inc(s_pad_set, 1)
            nc.gpsimd.memset(pad_row[:, :, D + 1], -1.0).then_inc(s_pad_set, 1)


            normalise(1, 0)

            def turn_pool(t):
                for j in range(2):
                    normalise2(t, j - 1)
                    if not missing(t, j + 3):
                        normalise(t + (j + 3) // 2, (j + 3) % 2)
                    scatter(t, j - 2)

            turn_pool(0)
            turn_pool(1)
            with pool.Fori(2, TURNS - 2) as t:
                turn_pool(t)
            turn_pool(TURNS - 2)
            turn_pool(TURNS - 1)
            for c in range(2):
                scatter(TURNS, c - 2)

            def scatter_tile(laps_done, b):
                pool.wait_ge(s_const, 11)
                pool.wait_ge(s_y[b], laps_done)
                for a in range(BLOCKS):
                    nc.gpsimd.indirect_dma_start(out=results, out_offset=bass.IndirectOffsetOnAxis(ap=to_i[:, b, a:a + 1], axis=0),
                                                 in_=t_y[:, b, a, :], in_offset=None).then_inc(s_ys[b], 16)

            for b in range(RING):
                scatter_tile(1, b)
            with pool.Fori(2, FULL_LAPS + 1) as laps_done:
                for b in range(RING):
                    scatter_tile(laps_done, b)
            for b in range(TILES % RING):
                scatter_tile(FULL_LAPS + 1, b)

            def add_both(lap, b):
                quad = bass.ds(lap * (SUM_RING * QUAD) + b * QUAD, QUAD)
                pool.wait_ge(s_const, 11)
                pool.wait_ge(s_second, lap * SUM_RING + (b + 1))
                nc.gpsimd.tensor_tensor(X[:, quad, :], X[:, quad, :], both[:, b, :, 0:D], ALU.add).then_inc(s_add, 1)

            with pool.Fori(0, QUADS // SUM_RING) as lap:
                for b in range(SUM_RING):
                    add_both(lap, b)

        @block.tensor
        def _(pe):
            mm = nc.tensor.matmul

            pe.wait_ge(s_w1, 16 * n_attn_weights)
            pe.wait_ge(s_bvw, 1)
            pe.wait_ge(s_ones, 1)
            pe.wait_ge(s_const, 2)
            mm(P[:, P_CTX, 0:D], bv_wide[:, :], wo[:, :], start=True, stop=False)
            mm(P[:, P_CTX, 0:D], ones_row[:, :], bo_row[:, :], start=False, stop=True)
            mm(P[:, P_CTX, R_LOGIT:R_RANK].rearrange("p (k e) -> p k e", e=E), ones_row[:, :],
               br_row[:, :].unsqueeze(1).to_broadcast([1, QUAD, E]), start=True, stop=True).then_inc(s_ab_mm, 1)

            def prep_xT(t, j):
                pe.wait_ge(s_xhat, t * 2 + j + 1)
                wait_from_one(pe, s_v, t * 2 + j)
                for k in range(QUAD):
                    last = nc.tensor.transpose(P[:, P_PREP, k * N:(k + 1) * N], xhat[:, k, :], ident[:, :])
                last.then_inc(s_xhatT, 1)

            def prep_q(t, j):
                pe.wait_ge(s_xT, t * 2 + j + 1)
                mm(P[:, P_PREP, :], wq[:, :], xT[:, :], start=True, stop=True).then_inc(s_qmm, 1)

            def prep_k(t, j):
                pe.wait_ge(s_q, t * 2 + j + 1)
                wait_from_one(pe, s_xn, t * 2 + (j - 2))
                mm(P[:, P_PREP, :], wk[:, :], xT[:, :], start=True, stop=True).then_inc(s_kmm, 1)

            def prep_v(t, j):
                pe.wait_ge(s_k, t * 2 + j + 1)
                for k in range(QUAD):
                    last = mm(P[:, P_PREP, k * N:(k + 1) * N], xT[:, k * N:(k + 1) * N], wv[:, :], start=True, stop=True)
                last.then_inc(s_vmm, 1)

            def scores(t, n, half):
                t, n = t + n // TURN, n % TURN
                j, k = n // QUAD, n % QUAD
                bank = P_SCORES + 2 * (n % 2) + half
                if half == 0:
                    wait_from_one(pe, s_sub, t * TURN + (n - 1))
                    pe.wait_ge(s_mask, t * 2 + j + 1)
                    pe.wait_ge(s_q, t * 2 + j + 1)
                    pe.wait_ge(s_kd[j], t * (16 * HEADS) + 16 * HEADS)
                bias = mask_bias[:, j, k, :].unsqueeze(1).to_broadcast([128, HALF, N])
                mm(P[:, bank, :].rearrange("p (h m) -> p h m", h=HALF), identb[:, :], bias, start=True, stop=False)
                mm(P[:, bank, :], qT[:, j, k * N:(k + 1) * N],
                   k_diag[:, j, k, half * HALF:(half + 1) * HALF, :].rearrange("p h m -> p (h m)"),
                   start=False, stop=True).then_inc(s_sc, 1)

            def turn_probs(t, n):
                pe.wait_ge(s_exp, t * TURN + n + 1)
                for half in range(2):
                    wait_from_one(pe, s_pTe, (t * TURN + n) * 2 + (half - 1))
                    for h in range(HALF):
                        last = nc.tensor.transpose(P[:, P_T + half, h * N:(h + 1) * N], probs[:, n % 2, half * HALF + h, :], ident[:, :])
                    last.then_inc(s_pT, 1)

            def context(t, n):
                pe.wait_ge(s_pTe, (t * TURN + n) * 2 + 2)
                pe.wait_ge(s_v, t * 2 + n // QUAD + 1)
                wait_from_one(pe, s_res, t * TURN + n)
                j, k = n // QUAD, n % QUAD
                if k == 0:
                    logits(t, j - 2)
                if k == 1 and not missing(t, j - 2):
                    pe.wait_ge(s_logit, upto(t, j - 2, 1, 1))
                if k == 2:
                    ranks(t, j - 2)
                if k == 3 and not missing(t, j - 2):
                    pe.wait_ge(s_rank_out, upto(t, j - 2, 1, 1))
                for h in range(HEADS):
                    slot, group = h % HALF, h // HALF
                    last = mm(P[slot * SLOT:(slot + 1) * SLOT, P_CTX, group * N:(group + 1) * N],
                              v_slots[:, n // QUAD, n % QUAD, h, :], probsT[:, h, :], start=True, stop=True,
                              tile_position=(0, slot * SLOT))
                last.then_inc(s_pv, 1)

            def context_back(g):
                pe.wait_ge(s_cr, g + 1)
                for group in range(2):
                    last = nc.tensor.transpose(P[:, P_CTX, group * 128:(group + 1) * 128], ctxT_raw[:, group * N:(group + 1) * N], ident[:, :])
                last.then_inc(s_back, 1)

            def context_turn(g):
                pe.wait_ge(s_norm, g + 1)
                nc.tensor.transpose(P[:, P_CTX, 0:N], ctxn[:, :, :].rearrange("p h d -> p (h d)"), ident[:, :]).then_inc(s_cT, 1)

            def project(g):
                pe.wait_ge(s_cTe, g + 1)
                mm(P[:, P_CTX, 0:D], ctxT[:, :], wo[:, :], start=True, stop=True).then_inc(s_wo, 1)

            def z_transposed(t, c):
                if missing(t, c):
                    return
                if not (isinstance(t, int) and 2 * t + c == QUADS - 1):
                    pe.wait_ge(s_z, upto(t, c, 1, 1))
                pe.wait_ge(s_v, upto(t, c, 1, 3) if not isinstance(t, int) else min(upto(t, c, 1, 3), QUADS))
                pe.wait_ge(s_q, upto(t, c, 1, 4) if not isinstance(t, int) else min(upto(t, c, 1, 4), QUADS))
                wait_from_one(pe, s_xn, upto(t, c))
                for k in range(QUAD):
                    last = nc.tensor.transpose(P[:, P_PREP, k * N:(k + 1) * N], rows_of(t, c)[:, k, 0:D], ident[:, :])
                last.then_inc(s_zT, 1)

            def logits(t, c, bank=P_CTX):
                if missing(t, c):
                    return
                pe.wait_ge(s_w2, 16 * n_expert_weights)
                pe.wait_ge(s_br, 1)
                pe.wait_ge(s_xn, upto(t, c, 1, 1))
                if bank == P_CTX:
                    wait_from_one(pe, s_rank_out, upto(t, c))
                for k in range(QUAD):
                    last = mm(P[:, bank, R_LOGIT + k * E:R_LOGIT + (k + 1) * E], xnT[:, k * N:(k + 1) * N], wr[:, :],
                              start=True, stop=True)
                last.then_inc(s_lg, 1)

            def ranks(t, c, bank=P_CTX):
                if missing(t, c):
                    return
                pe.wait_ge(s_const, 11)
                pe.wait_ge(s_pick, upto(t, c, 1, 1))
                wait_from_one(pe, s_place, upto(t, c))
                flat = picked[:, :, :].rearrange("p k e -> p (k e)")
                mm(P[:, bank, R_RANK:R_TOTAL], before[:, :], flat, start=True, stop=False, skip_group_check=True)
                for k in range(1, QUAD):
                    mm(P[:, bank, R_RANK + k * E:R_TOTAL], all_ones[:, :], flat[:, 0:(QUAD - k) * E], start=False,
                       stop=(k == QUAD - 1), skip_group_check=True)
                for k in range(QUAD):
                    last = mm(P[:, bank, R_TOTAL:R_TOTAL + E], all_ones[:, :], flat[:, k * E:(k + 1) * E], start=(k == 0),
                              stop=(k == QUAD - 1), skip_group_check=True)
                last.then_inc(s_rank, 1)

            def turn_pe(t, first, last):
                for n in range(TURN):
                    prev = not (first and n == 0)
                    more = not (last and n + 2 >= TURN)
                    turn_probs(t, n)
                    if prev:
                        context_back(t * TURN + (n - 1))
                    if more:
                        scores(t, n + 2, 0)
                    if n % QUAD == 0:
                        z_transposed(t, n // QUAD - 2)
                    if prev:
                        context_turn(t * TURN + (n - 1))
                    if more:
                        scores(t, n + 2, 1)
                    if prev:
                        project(t * TURN + (n - 1))
                    j, k = n // QUAD, n % QUAD
                    one, two = (t + (j + 1) // 2, (j + 1) % 2), (t + 1, j)
                    if k == 0 and not (last and j == 1):
                        prep_k(*one)
                    if k == 1 and not (last and j == 1):
                        prep_v(*one)
                    if k == 2 and not last:
                        prep_xT(*two)
                    if k == 3 and not last:
                        prep_q(*two)
                    context(t, n)

            prep_xT(0, 0)
            prep_q(0, 0)
            prep_k(0, 0)
            prep_v(0, 0)
            prep_xT(0, 1)
            prep_q(0, 1)
            for n in range(2):
                for half in range(2):
                    scores(0, n, half)
            turn_pe(0, True, False)
            turn_pe(1, False, False)
            with pe.Fori(2, TURNS - 1) as t:
                turn_pe(t, False, False)
            turn_pe(TURNS - 1, False, True)
            pe.wait_ge(s_sub, G)
            z_transposed(TURNS, -2)
            context_back(G - 1)
            logits(TURNS, -2, P_SCORES)
            context_turn(G - 1)
            project(G - 1)
            ranks(TURNS, -2, P_SCORES)
            pe.wait_ge(s_z_last, 1)
            z_transposed(TURNS, -1)
            logits(TURNS, -1, P_SCORES + 1)
            ranks(TURNS, -1, P_SCORES + 1)

            pe.wait_ge(s_res, G)
            pe.wait_ge(s_place, QUADS)

            def tile_transposed(lap, b):
                pe.wait_ge(s_load[b], lap * 16 + 16)
                wait_from_one(pe, s_txn, lap * RING + (b - 1))
                for a in range(BLOCKS):
                    last = nc.tensor.transpose(P[:, P_TT + b % 2, a * 128:(a + 1) * 128], t_row[:, b, a, 0:D], ident[:, :])
                last.then_inc(s_tT, 1)

            def tile_hidden(lap, b):
                pe.wait_ge(s_txn, lap * RING + (b + 1))
                pe.wait_ge(s_tw, lap * RING + (b + 1))
                wait_from_one(pe, s_tg, lap * RING + (b - 1))
                for c in range(CH):
                    mm(P[:, P_TH + b % 2 * CH + c, 0:TILE], tw[:, b, c * 128:(c + 1) * 128], t_xnT[:, b, :],
                       start=True, stop=True).then_inc(s_th, 1)

            def tile_result(lap, b):
                pe.wait_ge(s_tg, lap * RING + (b + 1))
                two = before_tile(lap, b, 2)
                wait_from_one(pe, s_y[two[1]], two[0] + 1)
                for a in range(BLOCKS):
                    for c in range(CH):
                        last = mm(P[:, P_TY + b % 2, a * D:(a + 1) * D], t_hid[:, b, c, a * 128:(a + 1) * 128],
                                  tw[:, b, EW_W2 + c * D:EW_W2 + (c + 1) * D], start=(c == 0), stop=(c == CH - 1))
                last.then_inc(s_ty, 1)

            def slot_pe(lap, b):
                for step, lag in ((tile_transposed, 0), (tile_hidden, 1), (tile_result, 2)):
                    tile = before_tile(lap, b, lag)
                    if not no_tile(*tile):
                        step(*tile)

            tile_slots(pe, slot_pe, 2)

        @block.scalar
        def _(act):
            fn = nc.scalar.activation
            nc.scalar.preload_act_table_set("natural_log_exp_and_others")

            def first_log_std(batch):
                graphs = first_norm[batch]
                act.wait_ge(s_var, batch + 1)
                fn(tmp_b[:, graphs], tmp_a[:, graphs], ACT.Ln).then_inc(s_lnv1, 1)
                act.wait_ge(s_lnv1, batch + 1)
                fn(tmp_c[:, graphs], tmp_b[:, graphs], ACT.Exp, scale=-0.5).then_inc(s_std, 1)

            first_log_std(0)
            act.wait_ge(s_w1, 16 * n_attn_weights)

            def prep_xT(t, j):
                act.wait_ge(s_xhatT, t * 2 + j + 1)
                wait_from_one(act, s_vmm, t * 2 + j)
                fn(xT[:, :], P[:, P_PREP, :], ACT.Identity).then_inc(s_xT, 1)

            def prep_q(t, j):
                act.wait_ge(s_qmm, t * 2 + j + 1)
                fn(qT[:, j, :], P[:, P_PREP, :], ACT.Identity, bias=bq_col[:, 0:1]).then_inc(s_q, 1)

            def prep_k(t, j):
                act.wait_ge(s_kmm, t * 2 + j + 1)
                if not (isinstance(t, int) and t == 0 and j == 0):
                    act.wait_ge(s_kd[1 - j], (t + (j - 1)) * (16 * HEADS) + 16 * HEADS if j == 0 else t * (16 * HEADS) + 16 * HEADS)
                fn(kT[:, :], P[:, P_PREP, :], ACT.Identity, bias=bk_col[:, 0:1]).then_inc(s_k, 1)

            def prep_v(t, j):
                act.wait_ge(s_vmm, t * 2 + j + 1)
                wait_from_one(act, s_pv, t * TURN + (QUAD * j - QUAD))
                fn(v_slots[:, j, :, :, 0:HD].rearrange("p k h d -> p (k h) d"),
                   P[:, P_PREP, :].rearrange("p (a d) -> p a d", d=HD), ACT.Identity).then_inc(s_v, 1)

            def exps(t, n):
                act.wait_ge(s_sub, t * TURN + n + 1)
                p = probs[:, n % 2].rearrange("p h m -> p (h m)")
                fn(p, p, ACT.Exp, scale=float(HD) ** -0.5).then_inc(s_exp, 1)

            def probs_out(t, n):
                wait_from_one(act, s_pv, t * TURN + n)
                for half in range(2):
                    act.wait_ge(s_pT, (t * TURN + n) * 2 + half + 1)
                    fn(probsT[:, half * HALF:(half + 1) * HALF, :].rearrange("p h m -> p (h m)"), P[:, P_T + half, :], ACT.Identity).then_inc(s_pTe, 1)

            def context_out(g):
                act.wait_ge(s_cT, g + 1)
                fn(ctxT[:, :], P[:, P_CTX, 0:N], ACT.Identity).then_inc(s_cTe, 1)

            def raw_out(t, n):
                act.wait_ge(s_pv, t * TURN + n + 1)
                fn(ctxT_raw[:, :], P[:, P_CTX, 0:2 * N], ACT.Identity).then_inc(s_cr, 1)

            def log_std(t, c):
                if missing(t, c):
                    return
                act.wait_ge(s_var2, upto(t, c, 1, 1))
                fn(ln_var[:, :], var2[:, :], ACT.Ln).then_inc(s_lnv, 1)
                act.wait_ge(s_lnv, upto(t, c, 1, 1))
                fn(guess[:, :], ln_var[:, :], ACT.Exp, scale=-0.5).then_inc(s_guess, 1)

            def exp_of_gap(t, c):
                if missing(t, c):
                    return
                act.wait_ge(s_gap, upto(t, c, 1, 1))
                fn(exp_gap[:, quad_of(t, c)], gap[:, :], ACT.Exp).then_inc(s_eg, 1)

            def xn_out(t, c):
                if missing(t, c):
                    return
                act.wait_ge(s_w2, 16 * n_expert_weights)
                act.wait_ge(s_zT, upto(t, c, 1, 1))
                wait_from_one(act, s_lg, upto(t, c))
                fn(xnT[:, :], P[:, P_PREP, :], ACT.Identity, bias=beta_col[:, 0:1], scale=gamma_col[:, 0:1]).then_inc(s_xn, 1)

            def turn_act(t, first, last):
                for n in range(TURN):
                    if n % QUAD == 1:
                        log_std(t, n // QUAD - 1)
                    probs_out(t, n)
                    if not (first and n == 0):
                        context_out(t * TURN + (n - 1))
                    j, k = n // QUAD, n % QUAD
                    if k == 0:
                        xn_out(t, j - 2)
                    if not (last and n + 1 >= TURN):
                        exps(t + (n + 1) // TURN, (n + 1) % TURN)
                    if k == 0 and not (last and j == 1):
                        prep_k(t + (j + 1) // 2, (j + 1) % 2)
                    if k == 2:
                        exp_of_gap(t, j - 2)
                    if k == 1 and not (last and j == 1):
                        prep_v(t + (j + 1) // 2, (j + 1) % 2)
                    if k == 2 and not last:
                        prep_xT(t + 1, j)
                    if k == 3 and not last:
                        prep_q(t + 1, j)
                    raw_out(t, n)

            prep_xT(0, 0)
            prep_q(0, 0)
            prep_k(0, 0)
            act.wait_ge(s_v_ones, 1)
            prep_v(0, 0)
            prep_xT(0, 1)
            prep_q(0, 1)
            first_log_std(1)
            exps(0, 0)
            turn_act(0, True, False)
            first_log_std(2)
            turn_act(1, False, False)
            with act.Fori(2, TURNS - 1) as t:
                turn_act(t, False, False)
            turn_act(TURNS - 1, False, True)
            xn_out(TURNS, -2)
            context_out(G - 1)
            log_std(TURNS, -1)
            exp_of_gap(TURNS, -2)
            xn_out(TURNS, -1)
            exp_of_gap(TURNS, -1)

            nc.scalar.preload_act_table(ACT.Gelu)

            def tile_xn(lap, b):
                act.wait_ge(s_tT, lap * RING + (b + 1))
                wait_from_one(act, s_th, (lap * RING + (b - RING + 1)) * CH)
                fn(t_xnT[:, b, :], P[:, P_TT + b % 2, 0:TILE], ACT.Identity, bias=beta_col[:, 0:1],
                   scale=gamma_col[:, 0:1]).then_inc(s_txn, 1)

            def tile_gelu(lap, b):
                wait_from_one(act, s_ty, lap * RING + (b - RING + 1))
                for c in range(CH):
                    act.wait_ge(s_th, lap * (RING * CH) + (b * CH + c + 1))
                    last = fn(t_hid[:, b, c, :], P[:, P_TH + b % 2 * CH + c, 0:TILE], ACT.Gelu,
                              bias=tw[:, b, EW_B1 + c:EW_B1 + c + 1])
                last.then_inc(s_tg, 1)

            def slot_act(lap, b):
                for step, lag in ((tile_xn, 0), (tile_gelu, 1)):
                    tile = before_tile(lap, b, lag)
                    if not no_tile(*tile):
                        step(*tile)

            tile_slots(act, slot_act, 1)

            act.wait_ge(s_gates, 1)

            def first_gated(lap, b):
                act.wait_ge(s_both[b], lap * 16 + 16)
                for k in range(QUAD):
                    first = both[:, b, k, 0:D]
                    last = fn(first, first, ACT.Identity, scale=gates[:, 0, bass.ds(lap * (SUM_RING * QUAD) + (b * QUAD + k), 1)])
                last.then_inc(s_first, 1)

            with act.Fori(0, QUADS // SUM_RING) as lap:
                for b in range(SUM_RING):
                    first_gated(lap, b)

        @block.vector
        def _(dve):
            v = nc.vector
            chain = [0]

            def then(ins):
                chain[0] += 1
                ins.then_inc(s_ln, 1)
                dve.wait_ge(s_ln, chain[0])

            v.memset(ones_row[:, :], 1.0).then_inc(s_ones, 1)

            def first_stats(graphs):
                for g in graphs:
                    if g % TURN == 0:
                        dve.wait_ge(s_x[g // TURN], 16)
                    v.bn_stats(stats[:, g, :], X[:, g, :]).then_inc(s_stat, 1)

            def first_variance(batch):
                gs = first_norm[batch]
                me, mo = stats[:, gs, 1], stats[:, gs, 4]
                dve.wait_ge(s_stat, gs.stop)
                v.tensor_tensor(tmp_a[:, gs], stats[:, gs, 2], stats[:, gs, 5], ALU.add)
                v.tensor_tensor(tmp_c[:, gs], me, mo, ALU.add)
                then(v.tensor_tensor(tmp_b[:, gs], me, mo, ALU.subtract))
                v.tensor_scalar(mean[:, gs], tmp_c[:, gs], 0.5, None, ALU.mult)
                then(v.scalar_tensor_tensor(out=tmp_b[:, gs], in0=tmp_b[:, gs], scalar=0.25, in1=tmp_b[:, gs],
                                            op0=ALU.mult, op1=ALU.mult))
                then(v.scalar_tensor_tensor(out=tmp_a[:, gs], in0=tmp_a[:, gs], scalar=1.0 / D, in1=tmp_b[:, gs],
                                            op0=ALU.mult, op1=ALU.add))
                v.tensor_scalar(tmp_a[:, gs], tmp_a[:, gs], EPS, None, ALU.add).then_inc(s_var, 1)

            def first_refine(batch):
                gs = first_norm[batch]
                dve.wait_ge(s_std, batch + 1)
                then(v.tensor_tensor(tmp_b[:, gs], tmp_c[:, gs], tmp_c[:, gs], ALU.mult))
                then(v.scalar_tensor_tensor(out=tmp_b[:, gs], in0=tmp_b[:, gs], scalar=-0.5, in1=tmp_a[:, gs],
                                            op0=ALU.mult, op1=ALU.mult))
                v.scalar_tensor_tensor(out=rstd[:, gs], in0=tmp_b[:, gs], scalar=1.5, in1=tmp_c[:, gs],
                                       op0=ALU.add, op1=ALU.mult).then_inc(s_rstd, 1)

            first_stats(range(TURN))
            first_variance(0)
            dve.wait_ge(s_w1, 16 * n_attn_weights)
            v.tensor_copy(bv_wide[:, :], bv_col[:, 0:1].to_broadcast([128, 128])).then_inc(s_bvw, 1)
            first_refine(0)
            then(v.memset(v_slots[:, :, :, :, :].rearrange("p b k h s -> p (b k h s)"), 0.0))
            v.memset(v_slots[:, :, :, :, HD:HD + 1].rearrange("p b k h s -> p (b k h) s"), 1.0).then_inc(s_v_ones, 1)
            dve.wait_ge(s_ab_mm, 1)
            v.tensor_copy(attn_bias[:, :], P[:, P_CTX, 0:D]).then_inc(s_ab, 1)
            v.tensor_copy(br_wide[:, :, :].rearrange("p k e -> p (k e)"), P[:, P_CTX, R_LOGIT:R_RANK]).then_inc(s_br, 1)

            def mask(t, j):
                dve.wait_ge(s_adj[j], t * 16 + 16)
                wait_from_one(dve, s_sc, t * 16 + (8 * j - 8))
                v.tensor_scalar(mask_bias[:, j], adj_raw[:, j], 0.0, MASKED, ALU.is_equal, ALU.mult).then_inc(s_mask, 1)

            def score_banks(n):
                first = P_SCORES + 2 * (n % 2)
                return P[:, first:first + 2, :].rearrange("p b (h m) -> p (b h) m", h=HALF)

            def maxima(t, n):
                dve.wait_ge(s_sc, (t * TURN + n) * 2 + 2)
                if n == 0:
                    wait_from_one(dve, s_edge, t)
                v.reduce_max(row_max[:, n, :], score_banks(n), AX).then_inc(s_max, 1)

            def less_max(t, n):
                dve.wait_ge(s_max, t * TURN + n + 1)
                wait_from_one(dve, s_pT, (t * TURN + n) * 2 - 2)
                m = row_max[:, n, :].unsqueeze(2).to_broadcast([128, HEADS, N])
                v.tensor_tensor(probs[:, n % 2], score_banks(n), m, ALU.subtract).then_inc(s_sub, 1)

            def normalise(g):
                dve.wait_ge(s_back, g + 1)
                back = P[:, P_CTX, 0:256].rearrange("p (h s) -> p h s", s=SLOT)
                v.reciprocal(rden[:, :], back[:, :, HD]).then_inc(s_rden, 1)
                dve.wait_ge(s_rden, g + 1)
                v.tensor_tensor(ctxn[:, :, :], back[:, :, 0:HD], rden[:, :].unsqueeze(2).to_broadcast([128, HEADS, HD]),
                                ALU.mult).then_inc(s_norm, 1)

            def residual(t, n):
                g = t * TURN + n
                dve.wait_ge(s_wo, g + 1)
                dve.wait_ge(s_xc, t * 2 + n // QUAD + 1)
                xg = X[:, bass.ds(g, 1), :].rearrange("p a d -> p (a d)")
                v.tensor_tensor(xg, P[:, P_CTX, 0:D], xg, ALU.add).then_inc(s_res, 1)

            def second_stats(t, n):
                g = t * TURN + n
                xg = X[:, bass.ds(g, 1), :].rearrange("p a d -> p (a d)")
                dve.wait_ge(s_ab, 1)
                dve.wait_ge(s_res, g + 1)
                v.bn_stats(stats2[:, n // QUAD, n % QUAD, :], xg).then_inc(s_st2, 1)

            def flag_rows(t):
                dve.wait_ge(s_max, t * TURN + TURN)
                v.tensor_scalar(no_edge[:, bass.ds(t * TURN, TURN)], row_max[:, :, 0], EMPTY_ROW, HUGE, ALU.is_le,
                                ALU.mult).then_inc(s_edge, 1)

            def variance(t, c):
                if missing(t, c):
                    return
                r = c % 2
                me, mo = stats2[:, r, :, 1], stats2[:, r, :, 4]
                dve.wait_ge(s_st2, upto(t, c, QUAD, QUAD))
                v.tensor_tensor(mean_gap[:, :], me, mo, ALU.subtract).then_inc(s_ln2, 1)
                v.tensor_tensor(m2_sum[:, :], stats2[:, r, :, 2], stats2[:, r, :, 5], ALU.add).then_inc(s_ln2, 1)
                v.tensor_tensor(mean_sum[:, :], me, mo, ALU.add).then_inc(s_ln2, 1)
                dve.wait_ge(s_ln2, upto(t, c, 7, 3))
                v.scalar_tensor_tensor(out=mean_gap[:, :], in0=mean_gap[:, :], scalar=0.25, in1=mean_gap[:, :],
                                       op0=ALU.mult, op1=ALU.mult).then_inc(s_ln2, 1)
                wait_from_one(dve, s_z, upto(t, c, 1, -1))
                v.tensor_scalar(mean2[:, r, :], mean_sum[:, :], 0.5, None, ALU.mult)
                dve.wait_ge(s_ln2, upto(t, c, 7, 4))
                v.scalar_tensor_tensor(out=m2_sum[:, :], in0=m2_sum[:, :], scalar=1.0 / D, in1=mean_gap[:, :],
                                       op0=ALU.mult, op1=ALU.add).then_inc(s_ln2, 1)
                dve.wait_ge(s_ln2, upto(t, c, 7, 5))
                v.tensor_scalar(var2[:, :], m2_sum[:, :], 1.0 + EPS, EPS * EPS, ALU.mult, ALU.add).then_inc(s_var2, 1)

            def refine(t, c):
                if missing(t, c):
                    return
                dve.wait_ge(s_guess, upto(t, c, 1, 1))
                dve.wait_ge(s_var2, upto(t, c, 1, 1))
                v.tensor_tensor(newton[:, :], guess[:, :], guess[:, :], ALU.mult).then_inc(s_ln2, 1)
                dve.wait_ge(s_ln2, upto(t, c, 7, 6))
                v.scalar_tensor_tensor(out=newton[:, :], in0=newton[:, :], scalar=-0.5, in1=var2[:, :],
                                       op0=ALU.mult, op1=ALU.mult).then_inc(s_ln2, 1)
                dve.wait_ge(s_ln2, upto(t, c, 7, 7))
                v.scalar_tensor_tensor(out=rstd2[:, c % 2, :], in0=newton[:, :], scalar=1.5, in1=guess[:, :],
                                       op0=ALU.add, op1=ALU.mult).then_inc(s_rstd2, 1)

            def logits_out(t, c, bank=P_CTX):
                if missing(t, c):
                    return
                dve.wait_ge(s_lg, upto(t, c, 1, 1))
                v.tensor_tensor(logit[:, :, :], P[:, bank, R_LOGIT:R_RANK].rearrange("p (k e) -> p k e", e=E),
                                br_wide[:, :, :], ALU.add).then_inc(s_logit, 1)

            def best_two(t, c):
                if missing(t, c):
                    return
                dve.wait_ge(s_br, 1)
                dve.wait_ge(s_logit, upto(t, c, 1, 1))
                for k in range(QUAD):
                    last = v.max(top[:, k, :], logit[:, k, :])
                last.then_inc(s_rt, 1)
                dve.wait_ge(s_rt, upto(t, c, 4, 1))
                wait_from_one(dve, s_eg, upto(t, c))
                v.tensor_tensor(gap[:, :], top[:, :, 1], top[:, :, 0], ALU.subtract).then_inc(s_gap, 1)
                for k in range(QUAD):
                    last = v.max_index(top_i[:, k, :], top[:, k, :], logit[:, k, :])
                last.then_inc(s_rt, 1)

            def picks(t, c):
                if missing(t, c):
                    return
                r = c % 2
                dve.wait_ge(s_rt, upto(t, c, 4, 2))
                v.tensor_copy(top_f[:, :, :], top_i[:, :, 0:2]).then_inc(s_rt, 1)
                dve.wait_ge(s_rt, upto(t, c, 4, 3))
                for i in range(2):
                    last = v.tensor_tensor(pick[:, i], iota_e[:, :].unsqueeze(1).to_broadcast([128, QUAD, E]),
                                           top_f[:, :, i].unsqueeze(2).to_broadcast([128, QUAD, E]), ALU.is_equal)
                last.then_inc(s_rt, 1)
                v.tensor_copy(rows_of(t, c)[:, :, D + 1], top_f[:, :, 0])
                dve.wait_ge(s_rt, upto(t, c, 4, 4))
                wait_from_one(dve, s_rank, upto(t, c))
                v.tensor_tensor(picked[:, :, :], pick[:, 0], pick[:, 1], ALU.add).then_inc(s_pick, 1)

            def ranks_out(t, c, bank=P_CTX):
                if missing(t, c):
                    return
                dve.wait_ge(s_rank, upto(t, c, 1, 1))
                v.tensor_copy(rank[:, :], P[:, bank, R_RANK:R_TOTAL + E]).then_inc(s_rank_out, 1)

            def places(t, c):
                if missing(t, c):
                    return
                dve.wait_ge(s_rank_out, upto(t, c, 1, 1))
                v.tensor_tensor(place[:, :, :], rank[:, 0:QUAD * E].rearrange("p (k e) -> p k e", e=E),
                                base[:, :].unsqueeze(1).to_broadcast([128, QUAD, E]), ALU.add).then_inc(s_pl, 1)
                dve.wait_ge(s_pl, upto(t, c, 4, 1))
                v.tensor_tensor(base[:, :], rank[:, QUAD * E:], base[:, :], ALU.add).then_inc(s_pl, 1)
                v.tensor_tensor(placed[:, :, :, :], pick[:, :, :, :], place[:, :, :].unsqueeze(1).to_broadcast([128, 2, QUAD, E]),
                                ALU.mult).then_inc(s_pl, 1)
                dve.wait_ge(s_pl, upto(t, c, 4, 3))
                v.reduce_sum(place_f[:, :, :], placed[:, :, :, :], AX).then_inc(s_pl, 1)
                dve.wait_ge(s_pl, upto(t, c, 4, 4))
                v.tensor_copy(place_i[:, c % 2], place_f[:, :, :]).then_inc(s_place, 1)

            def turn_dve(t, first, last):
                for n in range(TURN):
                    if n == TURN - 1:
                        flag_rows(t)
                    prev = not (first and n == 0)
                    more = not (last and n + 1 >= TURN)
                    nxt = (t + (n + 1) // TURN, (n + 1) % TURN)
                    j, k = n // QUAD, n % QUAD
                    if more:
                        maxima(*nxt)
                    if prev:
                        normalise(t * TURN + (n - 1))
                    if more:
                        less_max(*nxt)
                    if first and n < TURN - 2:
                        first_stats(range((n + 2) * TURN, (n + 3) * TURN))
                    if first and n == TURN - 2:
                        first_variance(2)
                    if k == 2:
                        picks(t, j - 2)
                    before = (t, n - 1) if n else (t - 1, TURN - 1)
                    if prev:
                        residual(*before)
                    if k == 1:
                        logits_out(t, j - 2)
                    if k == 3:
                        ranks_out(t, j - 2)
                    if prev:
                        second_stats(*before)
                    if k == 0:
                        variance(t, j - 1)
                    if k == 1:
                        best_two(t, j - 2)
                    if k == 2:
                        refine(t, j - 1)
                    if k == 3:
                        places(t, j - 2)
                    if k == 3 and not last:
                        mask(t + 1, j)

            mask(0, 0)
            mask(0, 1)
            v.memset(k_diag[:, 1].rearrange("p k h m -> p (k h m)"), 0.0).then_inc(s_kd_zero, 1)
            first_stats(range(TURN, 2 * TURN))
            first_variance(1)
            maxima(0, 0)
            less_max(0, 0)
            first_refine(1)
            dve.wait_ge(s_const, 11)
            then(v.tensor_copy(base[:, :], region[:, :]))
            turn_dve(0, True, False)
            first_refine(2)
            turn_dve(1, False, False)
            with dve.Fori(2, TURNS - 1) as t:
                turn_dve(t, False, False)
            turn_dve(TURNS - 1, False, True)
            normalise(G - 1)
            logits_out(TURNS, -2, P_SCORES)
            best_two(TURNS, -2)
            residual(TURNS - 1, TURN - 1)
            second_stats(TURNS - 1, TURN - 1)
            variance(TURNS, -1)
            picks(TURNS, -2)
            refine(TURNS, -1)
            dve.wait_ge(s_rstd2, QUADS)
            for k in range(QUAD):
                last = v.tensor_scalar(last_row[:, k, 0:D], X[:, G - QUAD + k, :], mean2[:, 1, k:k + 1],
                                       rstd2[:, 1, k:k + 1], ALU.subtract, ALU.mult)
            last.then_inc(s_z_last, 1)
            ranks_out(TURNS, -2, P_SCORES)
            places(TURNS, -2)
            logits_out(TURNS, -1, P_SCORES + 1)
            best_two(TURNS, -1)
            picks(TURNS, -1)
            ranks_out(TURNS, -1, P_SCORES + 1)
            dve.wait_ge(s_scat[1], 16 * 2 * QUAD * (QUADS // 2 - 1))
            places(TURNS, -1)

            tables = [0]

            def next_table(ins):
                tables[0] += 1
                ins.then_inc(s_tb, 1)
                dve.wait_ge(s_tb, tables[0])

            dve.wait_ge(s_pl, 4 * QUADS)
            v.tensor_copy(pad_i[:, :], base[:, :]).then_inc(s_pad, 1)
            next_table(v.scalar_tensor_tensor(out=count_i[:, :], in0=base[:, :], scalar=TILE - 1.0, in1=region[:, :],
                                              op0=ALU.add, op1=ALU.subtract))
            next_table(v.tensor_scalar(tiles_i[:, :], count_i[:, :], TILE.bit_length() - 1, None, ALU.logical_shift_right))
            next_table(v.tensor_copy(tiles_of[:, :], tiles_i[:, :]))
            v.tensor_scalar(skip[:, :], tiles_of[:, :], -float(TILE), float(REGION), ALU.mult, ALU.add)
            next_table(v.tensor_copy(tiles_upto[:, 0:1], tiles_of[:, 0:1]))
            for e in range(1, E):
                next_table(v.tensor_tensor(tiles_upto[:, e:e + 1], tiles_upto[:, e - 1:e], tiles_of[:, e:e + 1], ALU.add))
            v.tensor_scalar(tile_row[:, :], tile_no[:, :], float(TILE), None, ALU.mult)
            wide = [128, TILES, E]
            next_table(v.tensor_tensor(behind[:, 0], tile_no[:, :].unsqueeze(2).to_broadcast(wide),
                                       tiles_upto[:, :].unsqueeze(1).to_broadcast(wide), ALU.is_ge))
            v.reduce_sum(tile_e[:, :], behind[:, 0], AX)
            next_table(v.tensor_tensor(behind[:, 1], behind[:, 0], skip[:, :].unsqueeze(1).to_broadcast(wide), ALU.mult))
            next_table(v.reduce_sum(tile_skip[:, :], behind[:, 1], AX))
            v.tensor_tensor(tile_row_i[:, :], tile_row[:, :], tile_skip[:, :], ALU.add)
            v.tensor_scalar(tile_e_i[:, :], tile_e[:, :], float(E - 1), None, ALU.min).then_inc(s_tab, 1)
            dve.wait_ge(s_tab, 1)

            def tile_out(lap, b):
                dve.wait_ge(s_ty, lap * RING + (b + 1))
                dve.wait_ge(s_tw, lap * RING + (b + 1))
                dve.wait_ge(s_to, lap * RING + (b + 1))
                wait_from_one(dve, s_ys[b], lap * (16 * BLOCKS))
                v.tensor_copy(to_i[:, b], to_f[:, b])
                v.tensor_tensor(t_y[:, b], P[:, P_TY + b % 2, 0:TILE].rearrange("p (a d) -> p a d", d=D),
                                tw[:, b, EW_B2:EW_B2 + D].unsqueeze(1).to_broadcast([128, BLOCKS, D]), ALU.add).then_inc(s_y[b], 1)

            def tile_weights(lap, b, e):
                wait_from_one(dve, s_y[b], lap)
                wait_from_one(dve, s_ty, lap * RING + (b - RING + 1))
                v.tensor_copy(tw[:, b, :], ew[:, bass.ds(e, 1), :].rearrange("p a c -> p (a c)")).then_inc(s_tw, 1)

            def tile_to(lap, b):
                dve.wait_ge(s_load[b], lap * 16 + 16)
                wait_from_one(dve, s_y[b], lap)
                v.scalar_tensor_tensor(out=to_f[:, b], in0=t_row[:, b, :, D + 1], scalar=tile_e[:, bass.ds(lap * RING + b, 1)],
                                       in1=t_row[:, b, :, D], op0=ALU.not_equal, op1=ALU.add).then_inc(s_to, 1)

            def slot_dve(lap, b):
                if not no_tile(lap, b):
                    e = dve.value_load(tile_e_i[0:1, bass.ds(lap * RING + b, 1)], min_val=0, max_val=E - 1)
                ready = before_tile(lap, b, 3)
                if not no_tile(*ready):
                    tile_out(*ready)
                if not no_tile(lap, b):
                    tile_weights(lap, b, e)
                    tile_to(lap, b)

            tile_slots(dve, slot_dve, 3)

            gate_steps = [0]

            def next_gate(ins):
                gate_steps[0] += 1
                ins.then_inc(s_gt, 1)
                dve.wait_ge(s_gt, gate_steps[0])

            dve.wait_ge(s_eg, QUADS)
            dve.wait_ge(s_edge, TURNS)
            v.tensor_scalar(tmp_a[:, :], exp_gap[:, :], 1.0, None, ALU.add)
            next_gate(v.tensor_scalar(no_edge[:, :], no_edge[:, :], HUGE, 0.0, ALU.mult, ALU.mult))
            next_gate(v.reciprocal(tmp_b[:, :], tmp_a[:, :]))
            next_gate(v.tensor_tensor(gates[:, 0], tmp_b[:, :], no_edge[:, :], ALU.add))
            v.tensor_tensor(gates[:, 1], gates[:, 0], exp_gap[:, :], ALU.mult).then_inc(s_gates, 1)
            dve.wait_ge(s_gates, 1)

            def second_gated(lap, b):
                dve.wait_ge(s_first, lap * SUM_RING + (b + 1))
                for k in range(QUAD):
                    first = both[:, b, k, 0:D]
                    last = v.scalar_tensor_tensor(out=first, in0=both[:, b, k, D:2 * D],
                                                  scalar=gates[:, 1, bass.ds(lap * (SUM_RING * QUAD) + (b * QUAD + k), 1)],
                                                  in1=first, op0=ALU.mult, op1=ALU.add)
                last.then_inc(s_second, 1)

            with dve.Fori(0, QUADS // SUM_RING) as lap:
                for b in range(SUM_RING):
                    second_gated(lap, b)



_INS = ["x", "adj", "L0_gnn_Wq", "L0_gnn_bq", "L0_gnn_Wk", "L0_gnn_bk", "L0_gnn_Wv", "L0_gnn_bv", "L0_gnn_Wo",
        "L0_gnn_bo", "L0_ffn_gamma", "L0_ffn_beta", "L0_ffn_Wr", "L0_ffn_br", "L0_ffn_W1", "L0_ffn_b1", "L0_ffn_W2",
        "L0_ffn_b2"]


def kernel(**inputs):
    import numpy as _np
    import concourse.bacc as _bacc
    from concourse import mybir as _mybir
    from concourse.bass_utils import run_bass_kernel_spmd as _run

    nc = _bacc.Bacc("TRN2", target_bir_lowering=False, num_devices=1)
    arrays, args = {}, []
    for name in _INS:
        a = _np.ascontiguousarray(inputs[name])
        arrays[f"in_{name}_dram"] = a
        args.append(nc.dram_tensor(f"in_{name}_dram", a.shape, _mybir.dt.from_np(a.dtype), kind="ExternalInput").ap())
    out = nc.dram_tensor("out_0_dram", inputs["x"].shape, _mybir.dt.float32, kind="ExternalOutput").ap()
    build(nc, *args, out)
    r = _run(nc, [arrays], core_ids=[0])
    return r.results[0]["out_0_dram"]
```
